# Optimizing a Trainium2 kernel written in Bass

```python
import numpy as np
import jax
import jax.numpy as jnp

def _softmax(x, axis=-1):
    return jax.nn.softmax(x, axis=axis)

def _gelu(x):
    return jax.nn.gelu(x, approximate=True)

def _silu(x):
    return jax.nn.silu(x)

def _sigmoid(x):
    return jax.nn.sigmoid(x)

def _layernorm(x, axis=-1, eps=1e-05):
    m = jnp.mean(x, axis=axis, keepdims=True)
    v = jnp.var(x, axis=axis, keepdims=True)
    return (x - m) / jnp.sqrt(v + eps)

def _scatter_add(tgt, idx, src, axis=0):
    return tgt.at[idx].add(src)

def _segment_sum(src, seg, n):
    return jax.ops.segment_sum(src, seg, n)
kernel_name = 'mk_decoder_postln_d1_seqx_r8_ba1f30'

def setup_inputs(seed: int=0):
    np.random.seed(seed)
    _w = jnp.asarray

    def _rec_inputs():
        import jax
        import jax.numpy as jnp
        _rk = jax.random.key(seed)
        x = -0.0005146 + 1 * jax.random.normal(jax.random.fold_in(_rk, 1), (32, 64, 512), jnp.float32)
        _lenS = 64 - jax.random.randint(jax.random.fold_in(_rk, 7), (32,), 0, max(1, 64 // 4) + 1, jnp.int32)
        _lenS2 = 64 - jax.random.randint(jax.random.fold_in(_rk, 8), (32,), 0, max(1, 64 // 4) + 1, jnp.int32)
        _ctx_4096P = jax.random.normal(jax.random.fold_in(_rk, 11), (32, 16, 512), jnp.float32)
        _ctx_4096c = jax.random.dirichlet(jax.random.fold_in(_rk, 511), 0.3 * jnp.ones((16,), jnp.float32), (32, 64))
        _ctx_4096t = jnp.einsum('bsk,bkd->bsd', _ctx_4096c, _ctx_4096P)
        _ctx_4096t = _ctx_4096t * jax.lax.rsqrt(jnp.mean(jnp.square(_ctx_4096t)) + 1e-12) * 0.953939
        ctx_4096 = -0.000520686 + 1.00062 * (_ctx_4096t + 0.3 * jax.random.normal(jax.random.fold_in(_rk, 611), (32, 64, 512), jnp.float32))
        return (x, ctx_4096)
    x, ctx_4096 = _rec_inputs()

    def _L0_attn_setup():
        import jax, jax.numpy as jnp
        import numpy as np
        HIDDEN = 512
        NH = 32
        NKV = 8
        HD = 128
        GS = 128
        BASE = 10000.0
        B, S = (2, 256)

        def _dequant(codes, scales):
            w = codes.astype(jnp.float32) - 8.0
            return w * jnp.repeat(scales, GS, axis=0)

        def _rope(x):
            s, d = (x.shape[2], x.shape[3])
            pos = jnp.arange(s, dtype=jnp.float32)
            inv_freq = 1.0 / BASE ** (jnp.arange(0, d, 2, dtype=jnp.float32) / d)
            f = pos[:, None] * inv_freq[None, :]
            cos = jnp.cos(f)[None, None]
            sin = jnp.sin(f)[None, None]
            xe = x[..., ::2]
            xo = x[..., 1::2]
            re = xe * cos - xo * sin
            ro = xo * cos + xe * sin
            return jnp.stack([re, ro], axis=-1).reshape(x.shape)
        key = jax.random.key(seed)
        ks = jax.random.split(key, 9)

        def codes(k, i, o):
            return jax.random.randint(k, (i, o), 0, 16, dtype=jnp.int32)

        def scales(k, i, o):
            return jax.random.uniform(k, (i // GS, o), dtype=jnp.float32) * 0.02
        return {'hidden_states': jax.random.normal(ks[0], (B, S, HIDDEN), jnp.float32), 'q_codes': codes(ks[1], HIDDEN, NH * HD), 'q_scales': scales(ks[2], HIDDEN, NH * HD), 'k_codes': codes(ks[3], HIDDEN, NKV * HD), 'k_scales': scales(ks[4], HIDDEN, NKV * HD), 'v_codes': codes(ks[5], HIDDEN, NKV * HD), 'v_scales': scales(ks[6], HIDDEN, NKV * HD), 'o_codes': codes(ks[7], NH * HD, HIDDEN), 'o_scales': scales(ks[8], NH * HD, HIDDEN)}
    _L0_attn_all = _L0_attn_setup()
    _L0_attn_in = {k: v for k, v in _L0_attn_all.items() if k in ('q_codes', 'q_scales', 'k_codes', 'k_scales', 'v_codes', 'v_scales', 'o_codes', 'o_scales')}
    del _L0_attn_all

    def _L0_xattn_setup():
        import jax, jax.numpy as jnp
        import numpy as np
        B, C, N = (8, 64, 512)
        key = jax.random.key(seed)
        k1, k2, k3 = jax.random.split(key, 3)
        k = jax.random.normal(k1, (B, C, N), dtype=jnp.float32)
        q = jax.random.normal(k2, (B, C, N), dtype=jnp.float32)
        v = jax.random.normal(k3, (B, C, N), dtype=jnpp.float32) if False else jax.random.normal(k3, (B, C, N), dtype=jnp.float32)
        return {'k': k, 'q': q, 'v': v}
    _L0_xattn_all = _L0_xattn_setup()
    _L0_xattn_in = {k: v for k, v in _L0_xattn_all.items() if k in ()}
    del _L0_xattn_all

    def _L0_ffn_setup():
        import jax, jax.numpy as jnp
        import numpy as np
        HIDDEN = 512
        INTER = 1376
        SPARSITY = 0.5

        def _ternary_weight(key, out_dim, in_dim, sparsity):
            k_mask, k_sign = jax.random.split(key)
            nonzero = jax.random.bernoulli(k_mask, 1.0 - sparsity, (out_dim, in_dim))
            sign = jnp.where(jax.random.bernoulli(k_sign, 0.5, (out_dim, in_dim)), 1.0, -1.0)
            return (nonzero * sign).astype(jnp.float32)
        key = jax.random.key(seed)
        kx, kg, ku, kd, ksg, ksu, ksd = jax.random.split(key, 7)
        x = jax.random.normal(kx, (4, 256, HIDDEN), dtype=jnp.float32)
        Wg = _ternary_weight(kg, INTER, HIDDEN, SPARSITY)
        Wu = _ternary_weight(ku, INTER, HIDDEN, SPARSITY)
        Wd = _ternary_weight(kd, HIDDEN, INTER, SPARSITY)
        ag = jax.random.uniform(ksg, (INTER,), dtype=jnp.float32, minval=0.5, maxval=1.5) / np.sqrt(HIDDEN)
        au = jax.random.uniform(ksu, (INTER,), dtype=jnp.float32, minval=0.5, maxval=1.5) / np.sqrt(HIDDEN)
        ad = jax.random.uniform(ksd, (HIDDEN,), dtype=jnp.float32, minval=0.5, maxval=1.5) / np.sqrt(INTER)
        return {'x': x, 'Wg': Wg, 'Wu': Wu, 'Wd': Wd, 'ag': ag, 'au': au, 'ad': ad}
    _L0_ffn_all = _L0_ffn_setup()
    _L0_ffn_in = {k: v for k, v in _L0_ffn_all.items() if k in ('Wg', 'Wu', 'Wd', 'ag', 'au', 'ad')}
    del _L0_ffn_all
    return {'x': x, 'ctx_4096': ctx_4096, 'L0_attn_q_codes': _L0_attn_in['q_codes'], 'L0_attn_q_scales': _L0_attn_in['q_scales'], 'L0_attn_k_codes': _L0_attn_in['k_codes'], 'L0_attn_k_scales': _L0_attn_in['k_scales'], 'L0_attn_v_codes': _L0_attn_in['v_codes'], 'L0_attn_v_scales': _L0_attn_in['v_scales'], 'L0_attn_o_codes': _L0_attn_in['o_codes'], 'L0_attn_o_scales': _L0_attn_in['o_scales'], 'L0_ffn_Wg': _L0_ffn_in['Wg'], 'L0_ffn_Wu': _L0_ffn_in['Wu'], 'L0_ffn_Wd': _L0_ffn_in['Wd'], 'L0_ffn_ag': _L0_ffn_in['ag'], 'L0_ffn_au': _L0_ffn_in['au'], 'L0_ffn_ad': _L0_ffn_in['ad']}

def reference(x, ctx_4096, L0_attn_q_codes, L0_attn_q_scales, L0_attn_k_codes, L0_attn_k_scales, L0_attn_v_codes, L0_attn_v_scales, L0_attn_o_codes, L0_attn_o_scales, L0_ffn_Wg, L0_ffn_Wu, L0_ffn_Wd, L0_ffn_ag, L0_ffn_au, L0_ffn_ad):
    import jax
    import jax.numpy as jnp

    def _L0_attn_ref(hidden_states, q_codes, q_scales, k_codes, k_scales, v_codes, v_scales, o_codes, o_scales):
        import jax, jax.numpy as jnp
        import numpy as np
        HIDDEN = 512
        NH = 32
        NKV = 8
        HD = 128
        GS = 128
        BASE = 10000.0
        B, S = (2, 256)

        def _dequant(codes, scales):
            w = codes.astype(jnp.float32) - 8.0
            return w * jnp.repeat(scales, GS, axis=0)

        def _rope(x):
            s, d = (x.shape[2], x.shape[3])
            pos = jnp.arange(s, dtype=jnp.float32)
            inv_freq = 1.0 / BASE ** (jnp.arange(0, d, 2, dtype=jnp.float32) / d)
            f = pos[:, None] * inv_freq[None, :]
            cos = jnp.cos(f)[None, None]
            sin = jnp.sin(f)[None, None]
            xe = x[..., ::2]
            xo = x[..., 1::2]
            re = xe * cos - xo * sin
            ro = xo * cos + xe * sin
            return jnp.stack([re, ro], axis=-1).reshape(x.shape)
        b, s, _ = hidden_states.shape
        q = hidden_states @ _dequant(q_codes, q_scales)
        k = hidden_states @ _dequant(k_codes, k_scales)
        v = hidden_states @ _dequant(v_codes, v_scales)
        q = q.reshape(b, s, NH, HD).transpose(0, 2, 1, 3)
        k = k.reshape(b, s, NKV, HD).transpose(0, 2, 1, 3)
        v = v.reshape(b, s, NKV, HD).transpose(0, 2, 1, 3)
        q = _rope(q)
        k = _rope(k)
        rf = NH // NKV
        k = jnp.repeat(k, rf, axis=1)
        v = jnp.repeat(v, rf, axis=1)
        scale = HD ** (-0.5)
        causal = jnp.tril(jnp.ones((s, s), dtype=bool))
        mask = jnp.where(causal, 0.0, -jnp.inf).astype(q.dtype)
        scores = jnp.einsum('bhqd,bhkd->bhqk', q, k) * scale + mask[None, None]
        attn = jax.nn.softmax(scores, axis=-1)
        out = jnp.einsum('bhqk,bhkd->bhqd', attn, v)
        out = out.transpose(0, 2, 1, 3).reshape(b, s, NH * HD)
        return out @ _dequant(o_codes, o_scales)

    def _L0_xattn_ref(k, q, v):
        import jax, jax.numpy as jnp
        import numpy as np
        B, C, N = (8, 64, 512)
        input_dim = k.shape[1]
        scores = jnp.einsum('bcn,bcm->bnm', k, q) / jnp.sqrt(jnp.float32(input_dim))
        attn = jax.nn.softmax(scores, axis=-1)
        out = jnp.einsum('bnm,bcm->bcn', attn, v)
        return out

    def _L0_ffn_ref(x, Wg, Wu, Wd, ag, au, ad):
        import jax, jax.numpy as jnp
        import numpy as np
        HIDDEN = 512
        INTER = 1376
        SPARSITY = 0.5

        def _ternary_weight(key, out_dim, in_dim, sparsity):
            k_mask, k_sign = jax.random.split(key)
            nonzero = jax.random.bernoulli(k_mask, 1.0 - sparsity, (out_dim, in_dim))
            sign = jnp.where(jax.random.bernoulli(k_sign, 0.5, (out_dim, in_dim)), 1.0, -1.0)
            return (nonzero * sign).astype(jnp.float32)
        gate = jnp.einsum('bsh,ih->bsi', x, Wg) * ag
        up = jnp.einsum('bsh,ih->bsi', x, Wu) * au
        h = jax.nn.silu(gate) * up
        out = jnp.einsum('bsi,hi->bsh', h, Wd) * ad
        return out
    x = _layernorm(x + _L0_attn_ref(x, L0_attn_q_codes, L0_attn_q_scales, L0_attn_k_codes, L0_attn_k_scales, L0_attn_v_codes, L0_attn_v_scales, L0_attn_o_codes, L0_attn_o_scales), axis=-1)
    x = _layernorm(x + _L0_xattn_ref(ctx_4096, x, ctx_4096), axis=-1)
    x = _layernorm(x + _L0_ffn_ref(x, L0_ffn_Wg, L0_ffn_Wu, L0_ffn_Wd, L0_ffn_ag, L0_ffn_au, L0_ffn_ad), axis=-1)
    return x

_drawn_inputs = setup_inputs


def setup_inputs(seed=0):
    import zlib

    import numpy as np

    out = dict(_drawn_inputs(seed))
    spreads = {}
    factors = {}
    for name, (base, spread) in spreads.items():
        noise = np.random.default_rng([zlib.crc32(name.encode()), seed]).standard_normal(out[name].shape)
        drawn = base * np.exp(spread * noise) if base else spread * noise
        out[name] = jnp.asarray(drawn.astype(out[name].dtype))
    for name, factor in factors.items():
        out[name] = (out[name] * factor).astype(out[name].dtype)
    return out
```

```python
import numpy as np
from contextlib import ExitStack

import concourse.bass as bass
from concourse import mybir

F32 = mybir.dt.float32
F16 = mybir.dt.float16
BF16 = mybir.dt.bfloat16
I32 = mybir.dt.int32
ALU = mybir.AluOpType
ACT = mybir.ActivationFunctionType
AX = mybir.AxisListType

P = 128
BATCH, SEQ, HID = 32, 64, 512
NH, NKV, HD = 32, 8, 128
REP = NH // NKV
TOK = BATCH * SEQ
TILES = TOK // P
KC = HID // P
QKV = (REP + 2) * HD
ROT = (REP + 1) * HD
GROUP_W = KC * QKV + REP * HID
CHUNK = 640
NCHUNK = GROUP_W // CHUNK
UNITS = NKV * TILES
STEP = 4
INTER = 1376
IC = -(-INTER // P)
ILAST = INTER - (IC - 1) * P
FFN_W = 2 * KC * INTER + IC * HID
FCH = UNITS // STEP - TILES // STEP
WSCALE = 64.0
EPS = 1e-5


def in_range(n, lo, hi):
    return not isinstance(n, int) or lo <= n < hi


def last(end, step):
    return end - step + 1


def above(n, count):
    return not isinstance(n, int) or count > 0


def attention(nc, keep, x_nat, x_t, w_codes, w_scales, cos_d, sin_d, mask_d, ident_d, ffn_d):
    acc, xth, xtl, ffn_w, ident = keep["acc"], keep["xth"], keep["xtl"], keep["ffn_w"], keep["ident"]
    with ExitStack() as ctx:
        def sb(name, shape, dt):
            return ctx.enter_context(nc.sbuf_tensor(name, shape, dt))

        def pb(name, cols):
            return ctx.enter_context(nc.psum_tensor(name, [P, cols], F32))

        def sem(name):
            return ctx.enter_context(nc.semaphore(name))

        wh = sb("wh", [P, 2 * GROUP_W], F16)
        wl = sb("wl", [P, 2 * GROUP_W], F16)
        codes = sb("codes", [P, 2, CHUNK], I32)
        scales = sb("scales", [P, 2, CHUNK], F32)
        w32 = sb("w32", [P, 2, CHUNK], F32)
        ffn32 = sb("ffn32", [P, CHUNK], F32)
        xt32 = sb("xt32", [P, TOK], F32)
        cos = sb("cos", [P, ROT], F32)
        sin = sb("sin", [P, ROT], F32)
        mask32 = sb("mask32", [P, P], F32)
        mask = sb("mask", [P, REP * P], BF16)
        identb = sb("identb", [P, P], BF16)
        rot_c = sb("rot_c", [P, ROT], F32)
        rot_s = sb("rot_s", [P, ROT], F32)
        rot = sb("rot", [P, ROT], F32)
        qkh = sb("qkh", [P, ROT], F16)
        qkl = sb("qkl", [P, ROT], F16)
        vh = sb("vh", [P, 2, HD], F16)
        vl = sb("vl", [P, 2, HD], F16)
        negmax = sb("negmax", [P, 2, REP], F32)
        sums = sb("sums", [P, 2, REP], F32)
        inv = sb("inv", [P, 2, REP], F32)
        prob = sb("prob", [P, REP, P], F32)
        probn = sb("probn", [P, REP, P], F32)
        pth = sb("pth", [P, REP * P], F16)
        ptl = sb("ptl", [P, REP * P], F16)
        oth = sb("oth", [P, 2, REP * P], F16)
        otl = sb("otl", [P, 2, REP * P], F16)

        ps_qkv = pb("ps_qkv", 1024)
        ps_qk = pb("ps_qk", 1024)
        ps_s = pb("ps_s", 512)
        ps_p = pb("ps_p", 512)
        ps_o = pb("ps_o", 512)
        ps_out = pb("ps_out", 512)

        const_in = sem("const_in")
        xt_in = sem("xt_in")
        x_in = sem("x_in")
        chunk_in = [sem("chunk_in0"), sem("chunk_in1")]
        ffn_in = sem("ffn_in")
        consts = sem("consts")
        xth_ready, xtl_ready = sem("xth_ready"), sem("xtl_ready")
        w32_ready, wh_ready, wl_ready = sem("w32_ready"), sem("wh_ready"), sem("wl_ready")
        ffn_ready = sem("ffn_ready")
        qkv_done, qk_t, scores, p_t, pv_done, out_done = (
            sem("qkv_done"), sem("qk_t"), sem("scores"), sem("p_t"), sem("pv_done"), sem("out_done"))
        rot_parts, rotated = sem("rot_parts"), sem("rotated")
        qkh_ready, qkl_ready = sem("qkh_ready"), sem("qkl_ready")
        vh_ready, vl_ready = sem("vh_ready"), sem("vl_ready")
        max_ready, exp_ready, inv_ready, prob_ready = (
            sem("max_ready"), sem("exp_ready"), sem("inv_ready"), sem("prob_ready"))
        pth_ready, ptl_ready = sem("pth_ready"), sem("ptl_ready")
        oth_ready, otl_ready = sem("oth_ready"), sem("otl_ready")
        acc_added = sem("acc_added")

        def wcol(n, at):
            return (n // TILES) % 2 * GROUP_W + at

        def xcol(n):
            return n % TILES * P

        block = ctx.enter_context(nc.Block())

        @block.sync
        def _(sp):
            def load_chunk(c, buf):
                if above(c, c - 1):
                    sp.wait_ge(w32_ready, c - 1)
                sp.dma_start(codes[:, buf, :], w_codes[bass.ds(c, 1), :, :].rearrange("a p f -> p (a f)")
                             ).then_inc(chunk_in[buf], 16)
                sp.dma_start(scales[:, buf, :], w_scales[bass.ds(c, 1), :].to_broadcast([P, CHUNK])
                             ).then_inc(chunk_in[buf], 16)

            load_chunk(0, 0)
            load_chunk(1, 1)
            for dst, src in ((cos, cos_d), (sin, sin_d), (mask32, mask_d), (ident, ident_d)):
                sp.dma_start(dst[:], src).then_inc(const_in, 16)
            sp.dma_start(acc[:], x_nat.rearrange("t p f -> p t f")).then_inc(x_in, 16)
            with sp.Fori(2, last(NKV * NCHUNK, 2), 2) as c:
                load_chunk(c, 0)
                load_chunk(c + 1, 1)

        @block.gpsimd
        def _(pool):
            pool.dma_start(xt32[:], x_t[0, :, :]).then_inc(xt_in, 16)
            for k in range(1, KC):
                pool.wait_ge(xtl_ready, k)
                pool.dma_start(xt32[:], x_t[k, :, :]).then_inc(xt_in, 16)

            def slot(n, par, load_ffn):
                if load_ffn is not None:
                    if above(n, load_ffn):
                        pool.wait_ge(ffn_ready, load_ffn)
                    pool.dma_start(ffn32[:], ffn_d[bass.ds(load_ffn, 1), :, :].rearrange("a p f -> p (a f)")
                                   ).then_inc(ffn_in, 16)
                if in_range(n, 1, UNITS + 1):
                    pool.wait_ge(inv_ready, n)
                    if above(n, n - 1):
                        pool.wait_ge(p_t, n - 1)
                    nc.gpsimd.tensor_tensor(
                        probn[:], prob[:],
                        inv[:, 1 - par, :].unsqueeze(2).to_broadcast([P, REP, P]),
                        ALU.mult).then_inc(prob_ready, 1)
                if in_range(n, 0, UNITS):
                    pool.wait_ge(rot_parts, 2 * n + 2)
                    if above(n, n):
                        pool.wait_ge(qk_t, n)
                    nc.gpsimd.tensor_tensor(rot[:], rot_c[:], rot_s[:], ALU.add).then_inc(rotated, 1)

            def body(n0, ffn):
                for j in range(STEP):
                    slot(n0 + j, j % 2, n0 // STEP if ffn and j == 0 else None)

            body(0, True)
            with pool.Fori(STEP, last(UNITS - TILES, STEP), STEP) as n0:
                body(n0, True)
            with pool.Fori(UNITS - TILES, last(UNITS, STEP), STEP) as n0:
                body(n0, False)
            slot(UNITS, 0, None)

        @block.scalar
        def _(act):
            act.wait_ge(const_in, 64)
            nc.scalar.activation(identb[:], ident[:], ACT.Copy)
            nc.scalar.activation(mask[:].rearrange("p (h k) -> p h k", h=REP),
                                 mask32[:].unsqueeze(1).to_broadcast([P, REP, P]), ACT.Copy).then_inc(consts, 1)

            def chunk_high(c, buf):
                act.wait_ge(w32_ready, c + 1)
                nc.scalar.activation(wh[:, bass.ds(c % (2 * NCHUNK) * CHUNK, CHUNK)], w32[:, buf, :],
                                     ACT.Copy, scale=WSCALE).then_inc(wh_ready, 1)

            for c in range(NCHUNK):
                chunk_high(c, c % 2)
                if c % 2 == 1:
                    k = c // 2
                    act.wait_ge(xt_in, 16 * (k + 1))
                    nc.scalar.activation(xth[:, k, :], xt32[:], ACT.Copy).then_inc(xth_ready, 1)

            def slot(n, par, chunk, buf):
                if in_range(n, 1, UNITS + 1):
                    act.wait_ge(max_ready, n)
                    if above(n, n - 1):
                        act.wait_ge(prob_ready, n - 1)
                    for h in range(REP):
                        e = nc.scalar.activation(prob[:, h, :], ps_s[:, h * P:(h + 1) * P], ACT.Exp,
                                                 bias=negmax[:, 1 - par, h:h + 1],
                                                 accum_out=sums[:, 1 - par, h:h + 1])
                    e.then_inc(exp_ready, 1)
                if chunk is not None:
                    chunk_high(chunk, buf)
                if in_range(n, 1, UNITS + 1):
                    act.wait_ge(p_t, n)
                    if above(n, n - 1):
                        act.wait_ge(pv_done, n - 1)
                    nc.scalar.activation(pth[:], ps_p[:], ACT.Copy).then_inc(pth_ready, 1)
                if in_range(n, 0, UNITS):
                    act.wait_ge(rot_parts, 2 * n + 2)
                    if above(n, n - 1):
                        act.wait_ge(pv_done, n - 1)
                    nc.scalar.activation(vh[:, par, :], ps_qkv[:, ROT:QKV], ACT.Copy,
                                         scale=1.0 / WSCALE).then_inc(vh_ready, 1)
                if in_range(n, 1, UNITS + 1):
                    act.wait_ge(pv_done, n)
                    nc.scalar.activation(oth[:, 1 - par, :], ps_o[:], ACT.Copy).then_inc(oth_ready, 1)
                if in_range(n, 0, UNITS):
                    act.wait_ge(qk_t, n + 1)
                    nc.scalar.activation(qkh[:], ps_qk[:, 0:ROT], ACT.Copy).then_inc(qkh_ready, 1)

            def body(n0, chunks):
                for j in range(STEP):
                    slot(n0 + j, j % 2, n0 // 2 + NCHUNK + j // 2 if chunks and j % 2 == 0 else None, j // 2)
                    if chunks and j == 3:
                        act.wait_ge(ffn_in, n0 // STEP * 16 + 16)
                        nc.scalar.activation(ffn_w[:, bass.ds(n0 // STEP * CHUNK, CHUNK)], ffn32[:],
                                             ACT.Copy).then_inc(ffn_ready, 1)

            body(0, True)
            with act.Fori(STEP, last(UNITS - TILES, STEP), STEP) as n0:
                body(n0, True)
            with act.Fori(UNITS - TILES, last(UNITS, STEP), STEP) as n0:
                body(n0, False)
            slot(UNITS, 0, None, 0)

        @block.vector
        def _(dve):
            def dequantise(c, buf):
                dve.wait_ge(chunk_in[buf], c // 2 * 32 + 32)
                if above(c, c - 1):
                    dve.wait_ge(wh_ready, c - 1)
                    dve.wait_ge(wl_ready, c - 1)
                nc.vector.scalar_tensor_tensor(w32[:, buf, :], codes[:, buf, :], -8.0, scales[:, buf, :],
                                               ALU.add, ALU.mult).then_inc(w32_ready, 1)

            def chunk_low(c, buf):
                dve.wait_ge(wh_ready, c + 1)
                at = bass.ds(c % (2 * NCHUNK) * CHUNK, CHUNK)
                nc.vector.scalar_tensor_tensor(wl[:, at], w32[:, buf, :], WSCALE, wh[:, at],
                                               ALU.mult, ALU.subtract).then_inc(wl_ready, 1)

            dequantise(0, 0)
            for c in range(NCHUNK):
                if c + 1 < NCHUNK:
                    dequantise(c + 1, (c + 1) % 2)
                chunk_low(c, c % 2)
                if c % 2 == 1:
                    k = c // 2
                    dve.wait_ge(xth_ready, k + 1)
                    nc.vector.tensor_tensor(xtl[:, k, :], xt32[:], xth[:, k, :],
                                            ALU.subtract).then_inc(xtl_ready, 1)
            dve.wait_ge(x_in, 16)

            def slot(n, par, chunk, buf):
                if in_range(n, 1, UNITS + 1):
                    dve.wait_ge(scores, n)
                    nc.vector.tensor_reduce(negmax[:, 1 - par, :], ps_s[:].rearrange("p (h k) -> p h k", h=REP),
                                            AX.X, ALU.max, negate=True).then_inc(max_ready, 1)
                if chunk is not None:
                    if above(n, n):
                        dve.wait_ge(qkv_done, n)
                    if above(n, n - 2):
                        dve.wait_ge(out_done, n - 2)
                    dequantise(chunk, buf)
                if in_range(n, 3, UNITS + 3):
                    dve.wait_ge(out_done, n - 2)
                    if above(n, n - 3):
                        dve.wait_ge(acc_added, n - 3)
                    tile = acc[:, bass.ds((n + 2 * TILES - 3) % TILES, 1), :].rearrange("p a f -> p (a f)")
                    nc.vector.scalar_tensor_tensor(tile, ps_out[:], 1.0 / WSCALE, tile,
                                                   ALU.mult, ALU.add).then_inc(acc_added, 1)
                if in_range(n, 1, UNITS + 1):
                    dve.wait_ge(exp_ready, n)
                    nc.vector.reciprocal(inv[:, 1 - par, :], sums[:, 1 - par, :]).then_inc(inv_ready, 1)
                if in_range(n, 0, UNITS):
                    dve.wait_ge(qkv_done, n + 1)
                    if above(n, n):
                        dve.wait_ge(rotated, n)
                    nc.vector.tensor_tensor(rot_c[:], ps_qkv[:, 0:ROT], cos[:], ALU.mult).then_inc(rot_parts, 1)
                    src = ps_qkv[:, 0:ROT].rearrange("p (i two) -> p two i", two=2)
                    dst = rot_s[:].rearrange("p (i two) -> p two i", two=2)
                    tab = sin[:].rearrange("p (i two) -> p two i", two=2)
                    nc.vector.tensor_tensor(dst, src[:, ::-1, :], tab, ALU.mult).then_inc(rot_parts, 1)
                if in_range(n, 1, UNITS + 1):
                    dve.wait_ge(pth_ready, n)
                    nc.vector.tensor_tensor(ptl[:], ps_p[:], pth[:], ALU.subtract).then_inc(ptl_ready, 1)
                if in_range(n, 0, UNITS):
                    dve.wait_ge(vh_ready, n + 1)
                    if above(n, n - 1):
                        dve.wait_ge(pv_done, n - 1)
                    nc.vector.scalar_tensor_tensor(vl[:, par, :], ps_qkv[:, ROT:QKV], 1.0 / WSCALE,
                                                   vh[:, par, :], ALU.mult, ALU.subtract).then_inc(vl_ready, 1)
                if chunk is not None:
                    chunk_low(chunk, buf)
                if in_range(n, 1, UNITS + 1):
                    dve.wait_ge(oth_ready, n)
                    nc.vector.tensor_tensor(otl[:, 1 - par, :], ps_o[:], oth[:, 1 - par, :],
                                            ALU.subtract).then_inc(otl_ready, 1)
                if in_range(n, 0, UNITS):
                    dve.wait_ge(qkh_ready, n + 1)
                    nc.vector.tensor_tensor(qkl[:], ps_qk[:, 0:ROT], qkh[:], ALU.subtract).then_inc(qkl_ready, 1)

            def body(n0, chunks):
                for j in range(STEP):
                    slot(n0 + j, j % 2, n0 // 2 + NCHUNK + j // 2 if chunks and j % 2 == 0 else None, j // 2)

            body(0, True)
            with dve.Fori(STEP, last(UNITS - TILES, STEP), STEP) as n0:
                body(n0, True)
            with dve.Fori(UNITS - TILES, last(UNITS, STEP), STEP) as n0:
                body(n0, False)
            for n in range(UNITS, UNITS + 3):
                slot(n, n % 2, None, 0)

        @block.tensor
        def _(pe):
            pe.wait_ge(consts, 1)

            def slot(n, par):
                if in_range(n, 0, UNITS):
                    pe.wait_ge(wl_ready, n // TILES * NCHUNK + NCHUNK)
                    if isinstance(n, int) and n == 0:
                        pe.wait_ge(xtl_ready, KC)
                    if above(n, n):
                        pe.wait_ge(vl_ready, n)
                    for k in range(KC):
                        for w_at, width, ps_at in ((0, 512, 0), (512, QKV - 512, 512)):
                            at = bass.ds(wcol(n, k * QKV + w_at), width)
                            out = ps_qkv[:, ps_at:ps_at + width]
                            xh = xth[:, k, bass.ds(xcol(n), P)]
                            xl = xtl[:, k, bass.ds(xcol(n), P)]
                            nc.tensor.matmul(out, xh, wh[:, at], start=(k == 0), stop=False)
                            nc.tensor.matmul(out, xh, wl[:, at], start=False, stop=False)
                            m = nc.tensor.matmul(out, xl, wh[:, at], start=False, stop=(k == KC - 1))
                    m.then_inc(qkv_done, 1)
                if in_range(n, 1, UNITS + 1):
                    pe.wait_ge(prob_ready, n)
                    if above(n, n - 1):
                        pe.wait_ge(ptl_ready, n - 1)
                    for h in range(REP):
                        m = nc.tensor.transpose(ps_p[:, h * P:(h + 1) * P], probn[:, h, :], ident[:])
                    m.then_inc(p_t, 1)

                def project(h):
                    if not in_range(n, 2, UNITS + 2):
                        return
                    if h == 0:
                        pe.wait_ge(otl_ready, n - 1)
                        if above(n, n - 2):
                            pe.wait_ge(acc_added, n - 2)
                    w = bass.ds(wcol(n + 2 * TILES - 2, KC * QKV + h * HID), HID)
                    oh = oth[:, par, h * P:(h + 1) * P]
                    nc.tensor.matmul(ps_out[:], oh, wh[:, w], start=(h == 0), stop=False)
                    nc.tensor.matmul(ps_out[:], oh, wl[:, w], start=False, stop=False)
                    m = nc.tensor.matmul(ps_out[:], otl[:, par, h * P:(h + 1) * P], wh[:, w],
                                         start=False, stop=(h == REP - 1))
                    if h == REP - 1:
                        m.then_inc(out_done, 1)

                project(0)
                project(1)
                if in_range(n, 1, UNITS + 1):
                    pe.wait_ge(pth_ready, n)
                    pe.wait_ge(vl_ready, n)
                    if above(n, n - 1):
                        pe.wait_ge(otl_ready, n - 1)
                    nc.tensor.matmul(ps_o[:], vh[:, 1 - par, :], pth[:], start=True, stop=False)
                    nc.tensor.matmul(ps_o[:], vl[:, 1 - par, :], pth[:], start=False, stop=False)
                    pe.wait_ge(ptl_ready, n)
                    nc.tensor.matmul(ps_o[:], vh[:, 1 - par, :], ptl[:], start=False,
                                     stop=True).then_inc(pv_done, 1)
                project(2)
                if in_range(n, 0, UNITS):
                    pe.wait_ge(rotated, n + 1)
                    if above(n, n):
                        pe.wait_ge(qkl_ready, n)
                    for h in range(REP + 1):
                        m = nc.tensor.transpose(ps_qk[:, h * P:(h + 1) * P], rot[:, h * P:(h + 1) * P], ident[:])
                    m.then_inc(qk_t, 1)
                project(3)
                if in_range(n, 0, UNITS):
                    if above(n, n):
                        pe.wait_ge(exp_ready, n)
                    nc.tensor.matmul(ps_s[:], identb[:], mask[:], start=True, stop=False)
                    kcol = slice(REP * P, ROT)
                    pe.wait_ge(qkh_ready, n + 1)
                    for h in range(REP):
                        c = slice(h * P, (h + 1) * P)
                        nc.tensor.matmul(ps_s[:, c], qkh[:, c], qkh[:, kcol], start=False, stop=False)
                    pe.wait_ge(qkl_ready, n + 1)
                    for h in range(REP):
                        c = slice(h * P, (h + 1) * P)
                        nc.tensor.matmul(ps_s[:, c], qkh[:, c], qkl[:, kcol], start=False, stop=False)
                        m = nc.tensor.matmul(ps_s[:, c], qkl[:, c], qkh[:, kcol], start=False,
                                             stop=(h == REP - 1))
                    m.then_inc(scores, 1)

            for n in range(STEP):
                slot(n, n % 2)
            with pe.Fori(STEP, last(UNITS, STEP), STEP) as n0:
                for j in range(STEP):
                    slot(n0 + j, j % 2)
            for n in range(UNITS, UNITS + 2):
                slot(n, n % 2)


def norm_statistics(nc, dve, act_wait, acc, stats, meanvar, rstd, work, sem_dve, count):
    with dve.Fori(0, TILES, 1) as t:
        nc.vector.bn_stats(stats[:, bass.ds(t, 1), :].rearrange("p a f -> p (a f)"),
                           acc[:, bass.ds(t, 1), :].rearrange("p a f -> p (a f)")).then_inc(sem_dve, 1)
    count += TILES
    dve.wait_ge(sem_dve, count)
    for t in range(TILES):
        nc.vector.bn_aggr(meanvar[:, t, :], stats[:, t, :]).then_inc(sem_dve, 1)
    count += TILES
    dve.wait_ge(sem_dve, count)
    nc.vector.tensor_scalar(work[:, 0, :], meanvar[:, :, 1], EPS, None, ALU.add).then_inc(sem_dve, 1)
    return count + 1


def norm_rstd(nc, dve, rstd, work, sem_dve, count):
    def step(ins, n):
        ins.then_inc(sem_dve, 1)
        dve.wait_ge(sem_dve, n)

    v, root, r, a = (work[:, i, :] for i in range(4))
    step(nc.vector.reciprocal(r, root), count + 1)
    step(nc.vector.tensor_tensor(a, r, r, ALU.mult), count + 2)
    step(nc.vector.tensor_tensor(root, a, v, ALU.mult), count + 3)
    step(nc.vector.tensor_scalar(a, root, -0.5, 1.5, ALU.mult, ALU.add), count + 4)
    step(nc.vector.tensor_tensor(rstd[:], r, a, ALU.mult), count + 5)
    return count + 5


def normalise(nc, out, tile, meanvar, rstd, t):
    mean = meanvar[:, bass.ds(t, 1), 0:1].rearrange("p a f -> p (a f)")
    return nc.vector.tensor_scalar(out, tile, mean, rstd[:, bass.ds(t, 1)], ALU.subtract, ALU.mult)


def cross_attention(nc, keep, ctx_nat, ctx_t):
    acc, ident = keep["acc"], keep["ident"]
    SCALE = float(SEQ) ** -0.5
    VC = SEQ + 1
    FILLS = 7
    with ExitStack() as ctx:
        def sb(name, shape, dt):
            return ctx.enter_context(nc.sbuf_tensor(name, shape, dt))

        def pb(name, cols, dt=F32):
            return ctx.enter_context(nc.psum_tensor(name, [P, cols], dt))

        def sem(name):
            return ctx.enter_context(nc.semaphore(name))

        stats = sb("stats1", [P, TILES, 6], F32)
        meanvar = sb("meanvar1", [P, TILES, 2], F32)
        work = sb("work1", [P, 4, TILES], F32)
        rstd = sb("rstd1", [P, TILES], F32)
        identh = sb("identh", [P, P], F16)
        ct32 = sb("ct32", [P, 2, TOK], F32)
        vth = sb("vth", [P, KC, BATCH, VC], F16)
        vtl = sb("vtl", [P, KC, BATCH, SEQ], F16)
        ctx32 = sb("ctx32", [P, 2, HID], F32)
        q_pair = sb("q_pair", [P, 4, HID], F16)
        k_pair = sb("k_pair", [P, 4, HID], F16)
        q_high = sb("q_high", [P, 4, HID], F16)
        k_low = sb("k_low", [P, 4, HID], F16)
        negmax = sb("negmax1", [P, 2, KC], F32)
        negmax_parts = sb("negmax_parts", [P, 2, KC, 2], F16)
        e32 = sb("e32", [P, 2, HID], F32)
        ph = sb("ph", [P, 2, KC, HID], F16)
        pl = sb("pl", [P, 2, KC, HID], F16)
        inv = sb("inv1", [P, 2, KC], F32)
        un = sb("un", [P, 2, KC, P], F32)

        ps_s = [pb("ps_smax0", HID), pb("ps_smax1", HID)]
        ps_e = [pb("ps_e0", HID), pb("ps_e1", HID)]
        ps_v = [pb("ps_v0", HID), pb("ps_v1", HID)]
        ps_n = pb("ps_n", 1024, F16)
        ps_x = pb("ps_x", HID)

        stat = sem("stat1")
        root = sem("root1")
        ct_in = [sem("ct_in0"), sem("ct_in1")]
        vth_ready, vtl_ready = sem("vth_ready"), sem("vtl_ready")
        ctx_in = [sem("ctx_in0"), sem("ctx_in1")]
        fills = sem("fills")
        ident_ready = sem("ident_ready")
        x1_ready = sem("x1_ready")
        high_ready, low_ready = sem("high_ready"), sem("low_ready")
        smax_done, max_ready, parts_ready, parts_t, row_ready = (
            sem("smax_done"), sem("max_ready1"), sem("parts_ready"), sem("parts_t"), sem("row_ready"))
        s_done, exp_ready, ph_ready, pl_ready = sem("s_done"), sem("exp_ready1"), sem("ph_ready"), sem("pl_ready")
        pv_done, inv_ready, un_ready, un_t, x_added = (
            sem("pv_done1"), sem("inv_ready1"), sem("un_ready"), sem("un_t"), sem("x_added"))

        def mine(b):
            return slice(0, SEQ) if b % 2 == 0 else slice(SEQ, P)

        def other(b):
            return slice(SEQ, P) if b % 2 == 0 else slice(0, SEQ)

        block = ctx.enter_context(nc.Block())

        def run(eng, slot, first, end):
            for s in range(first, 4):
                slot(s, s % 4)
            with eng.Fori(4, last(BATCH - 4, 4), 4) as s0:
                for j in range(4):
                    slot(s0 + j, j)
            for s in range(BATCH - 4, end):
                slot(s, s % 4)

        @block.sync
        def _(sp):
            for k in range(KC):
                if k >= 2:
                    sp.wait_ge(vtl_ready, k - 1)
                sp.dma_start(ct32[:, k % 2, :], ctx_t[k, :, :]).then_inc(ct_in[k % 2], 16)

            def load(t, buf):
                if above(t, 2 * t - 2):
                    sp.wait_ge(low_ready, 2 * t - 2)
                sp.dma_start(ctx32[:, buf, :], ctx_nat[bass.ds(t, 1), :, :].rearrange("a p f -> p (a f)")
                             ).then_inc(ctx_in[buf], 16)

            load(0, 0)
            load(1, 1)
            with sp.Fori(2, last(TILES, 2), 2) as t:
                load(t, 0)
                load(t + 1, 1)

        @block.gpsimd
        def _(pool):
            filled = 0
            for what, value in [(q_high[:], 0.0), (k_low[:], 0.0), (vth[:, :, :, SEQ:VC], 1.0)] + [
                    (q_high[other(i).start:other(i).start + 2, i, :], 1.0) for i in range(4)]:
                if filled:
                    pool.wait_ge(fills, filled)
                nc.gpsimd.memset(what, value).then_inc(fills, 1)
                filled += 1

            def slot(s, j):
                if in_range(s, 2, BATCH + 2):
                    for mc in range(KC):
                        pool.wait_ge(ph_ready, (s - 2) * KC + mc + 1)
                        nc.gpsimd.tensor_tensor(pl[:, j % 2, mc, :], e32[:, mc % 2, :], ph[:, j % 2, mc, :],
                                                ALU.subtract).then_inc(pl_ready, 1)

            run(pool, slot, 0, BATCH + 2)

        @block.scalar
        def _(act):
            nc.scalar.activation(identh[:], ident[:], ACT.Copy).then_inc(ident_ready, 1)
            for k in range(KC):
                act.wait_ge(ct_in[k % 2], 16 * (k // 2 + 1))
                nc.scalar.activation(vth[:, k, :, 0:SEQ], ct32[:, k % 2, :].rearrange("p (b c) -> p b c", b=BATCH),
                                     ACT.Copy).then_inc(vth_ready, 1)
            act.wait_ge(stat, 2 * TILES + 1)
            nc.scalar.activation(work[:, 1, :], work[:, 0, :], ACT.Sqrt).then_inc(root, 1)

            def prepare(b, j, part):
                i = j % 4
                if part == 0:
                    act.wait_ge(x1_ready, b // 2 + 1)
                    if above(b, KC * (b - 3)):
                        act.wait_ge(s_done, KC * (b - 3))
                    nc.scalar.activation(q_pair[mine(j), i, :], acc[mine(j), bass.ds(b // 2, 1), :]
                                         .rearrange("p a f -> p (a f)"), ACT.Copy)
                    return
                if part == 1:
                    act.wait_ge(ctx_in[j // 2], b // 4 * 16 + 16)
                half = mine(j) if part == 1 else other(j)
                e = nc.scalar.activation(k_pair[half, i, :], ctx32[mine(j), j // 2, :], ACT.Copy)
                if part == 2:
                    e.then_inc(high_ready, 1)

            for part in range(3):
                prepare(0, 0, part)

            def slot(s, j):
                for mc in range(KC):
                    if in_range(s, 2, BATCH + 2):
                        c = (s - 2) * KC + mc
                        act.wait_ge(s_done, c + 1)
                        if above(c, c - 1):
                            act.wait_ge(pl_ready, c - 1)
                        nc.scalar.activation(e32[:, mc % 2, :], ps_e[mc % 2][:], ACT.Exp,
                                             scale=SCALE).then_inc(exp_ready, 1)
                        if mc == 0 and above(s, s - 3):
                            act.wait_ge(pv_done, s - 3)
                        act.wait_ge(exp_ready, c + 1)
                        nc.scalar.activation(ph[:, j % 2, mc, :], e32[:, mc % 2, :], ACT.Copy).then_inc(ph_ready, 1)
                    if mc < 3 and in_range(s, 0, BATCH - 1):
                        prepare(s + 1, (j + 1) % 4, mc)

            run(act, slot, 0, BATCH + 2)

        @block.vector
        def _(dve):
            norm_statistics(nc, dve, None, acc, stats, meanvar, rstd, work, stat, 0)
            for k in range(KC):
                dve.wait_ge(vth_ready, k + 1)
                nc.vector.tensor_tensor(vtl[:, k, :, :], ct32[:, k % 2, :].rearrange("p (b c) -> p b c", b=BATCH),
                                        vth[:, k, :, 0:SEQ], ALU.subtract).then_inc(vtl_ready, 1)
            dve.wait_ge(root, 1)
            norm_rstd(nc, dve, rstd, work, stat, 2 * TILES + 1)

            def norm(t):
                tile = acc[:, bass.ds(t, 1), :].rearrange("p a f -> p (a f)")
                normalise(nc, tile, tile, meanvar, rstd, t).then_inc(x1_ready, 1)

            norm(0)
            norm(1)
            dve.wait_ge(fills, FILLS)

            def prepare(b, j, part):
                i = j % 4
                if part == 0:
                    dve.wait_ge(high_ready, b + 1)
                    dve.wait_ge(x1_ready, b // 2 + 1)
                    nc.vector.tensor_tensor(q_pair[other(j), i, :], acc[mine(j), bass.ds(b // 2, 1), :]
                                            .rearrange("p a f -> p (a f)"), q_pair[mine(j), i, :], ALU.subtract)
                elif part == 1:
                    nc.vector.tensor_tensor(k_low[mine(j), i, :], ctx32[mine(j), j // 2, :],
                                            k_pair[mine(j), i, :], ALU.subtract)
                else:
                    nc.vector.tensor_copy(q_high[mine(j), i, :], q_pair[mine(j), i, :]).then_inc(low_ready, 1)

            for part in range(3):
                prepare(0, 0, part)

            def slot(s, j):
                if in_range(s, 1, BATCH + 1):
                    dve.wait_ge(parts_t, s)
                    b1 = (j - 1) % 4
                    at = other(b1).start
                    nc.vector.tensor_copy(k_low[at:at + 2, b1, :], ps_n[0:2, 0:HID]).then_inc(row_ready, 1)
                if j % 2 == 1 and in_range(s, 0, BATCH - 4):
                    norm((s + 3) // 2)
                for mc in range(KC):
                    if in_range(s, 0, BATCH):
                        dve.wait_ge(smax_done, s * KC + mc + 1)
                        nc.vector.tensor_reduce(negmax[:, j % 2, mc:mc + 1], ps_s[mc % 2][:], AX.X, ALU.max,
                                                negate=True).then_inc(max_ready, 1)
                    if mc < 3 and in_range(s, 0, BATCH - 1):
                        prepare(s + 1, (j + 1) % 4, mc)
                if in_range(s, 0, BATCH):
                    dve.wait_ge(max_ready, KC * (s + 1))
                    if above(s, s - 1):
                        dve.wait_ge(parts_t, s - 1)
                    nc.vector.tensor_copy(negmax_parts[:, j % 2, :, 0], negmax[:, j % 2, :]).then_inc(parts_ready, 1)
                    dve.wait_ge(parts_ready, 2 * s + 1)
                    nc.vector.tensor_tensor(negmax_parts[:, j % 2, :, 1], negmax[:, j % 2, :],
                                            negmax_parts[:, j % 2, :, 0], ALU.subtract).then_inc(parts_ready, 1)
                if j % 2 == 1 and in_range(s, 5, BATCH + 5):
                    t = (s - 5) // 2
                    dve.wait_ge(un_t, t + 1)
                    tile = acc[:, bass.ds(t, 1), :].rearrange("p a f -> p (a f)")
                    nc.vector.tensor_tensor(tile, ps_x[:], tile, ALU.add).then_inc(x_added, 1)
                if in_range(s, 3, BATCH + 3):
                    b3 = (j - 3) % 4
                    dve.wait_ge(pv_done, s - 2)
                    v = ps_v[b3 % 2][:, 0:KC * VC].rearrange("p (n c) -> p n c", n=KC)
                    nc.vector.reciprocal(inv[:, b3 % 2, :], v[:, :, SEQ]).then_inc(inv_ready, 1)
                    dve.wait_ge(inv_ready, s - 2)
                    at = SEQ * (b3 % 2)
                    nc.vector.tensor_tensor(un[:, b3 // 2, :, at:at + SEQ], v[:, :, 0:SEQ],
                                            inv[:, b3 % 2, :].unsqueeze(2).to_broadcast([P, KC, SEQ]),
                                            ALU.mult).then_inc(un_ready, 1)

            run(dve, slot, 0, BATCH + 4)

        @block.tensor
        def _(pe):
            pe.wait_ge(fills, FILLS)
            pe.wait_ge(ident_ready, 1)

            def attend(s, j, n):
                if not in_range(s, 3, BATCH + 3):
                    return
                b3 = (j - 3) % 4
                if n == 0:
                    pe.wait_ge(pl_ready, KC * (s - 2))
                    if isinstance(s, int) and s == 3:
                        pe.wait_ge(vtl_ready, KC)
                    if above(s, s - 4):
                        pe.wait_ge(un_ready, s - 4)
                out = ps_v[b3 % 2]
                cols = slice(n * P, (n + 1) * P)
                for mc in range(KC):
                    full, part = out[:, n * VC:(n + 1) * VC], out[:, n * VC:n * VC + SEQ]
                    high = vth[:, mc, bass.ds(s - 3, 1), :].rearrange("p a c -> p (a c)")
                    low = vtl[:, mc, bass.ds(s - 3, 1), :].rearrange("p a c -> p (a c)")
                    p_high, p_low = ph[:, b3 % 2, mc, cols], pl[:, b3 % 2, mc, cols]
                    nc.tensor.matmul(full, p_high, high, start=(mc == 0), stop=False)
                    nc.tensor.matmul(part, p_high, low, start=False, stop=False)
                    m = nc.tensor.matmul(full, p_low, high, start=False, stop=(mc == KC - 1))
                if n == KC - 1:
                    m.then_inc(pv_done, 1)

            def slot(s, j):
                if in_range(s, 1, BATCH + 1):
                    pe.wait_ge(parts_ready, 2 * s)
                    if above(s, s - 1):
                        pe.wait_ge(row_ready, s - 1)
                    for n in range(KC):
                        m = nc.tensor.transpose(ps_n[0:2, n * P:(n + 1) * P],
                                                negmax_parts[:, (j - 1) % 2, n, :], identh[:])
                    m.then_inc(parts_t, 1)
                for mc in range(KC):
                    cols = slice(mc * P, (mc + 1) * P)
                    if in_range(s, 2, BATCH + 2):
                        i = (j - 2) % 4
                        if mc == 0:
                            pe.wait_ge(row_ready, s - 1)
                        c = (s - 2) * KC + mc
                        if above(c, c - 1):
                            pe.wait_ge(exp_ready, c - 1)
                        nc.tensor.matmul(ps_e[mc % 2][:], q_pair[:, i, cols], k_pair[:, i, :], start=True, stop=False)
                        nc.tensor.matmul(ps_e[mc % 2][:], q_high[:, i, cols], k_low[:, i, :], start=False,
                                         stop=True).then_inc(s_done, 1)
                    if in_range(s, 0, BATCH):
                        if mc == 0:
                            pe.wait_ge(low_ready, s + 1)
                        c = s * KC + mc
                        if above(c, c - 1):
                            pe.wait_ge(max_ready, c - 1)
                        nc.tensor.matmul(ps_s[mc % 2][:], k_pair[:, j, cols], q_pair[:, j, :], start=True,
                                         stop=True).then_inc(smax_done, 1)
                    if mc == 1:
                        attend(s, j, 0)
                        attend(s, j, 1)
                        if j % 2 == 1 and in_range(s, 5, BATCH + 5):
                            t = (s - 5) // 2
                            pe.wait_ge(un_ready, s - 3)
                            if above(s, t):
                                pe.wait_ge(x_added, t)
                            for n in range(KC):
                                m = nc.tensor.transpose(ps_x[:, n * P:(n + 1) * P],
                                                        un[:, ((j - 5) % 4) // 2, n, :], ident[:])
                            m.then_inc(un_t, 1)
                attend(s, j, 2)
                attend(s, j, 3)

            run(pe, slot, 0, BATCH + 4)


def feed_forward(nc, keep, ag_d, au_d, ad_d, out_d):
    acc, xth, xtl, ffn_w, ident = keep["acc"], keep["xth"], keep["xtl"], keep["ffn_w"], keep["ident"]
    GROUPS = TOK // 512
    GT = TILES // GROUPS
    w_gate = ffn_w[:, 0:KC * INTER].rearrange("p (k i) -> p k i", k=KC)
    w_up = ffn_w[:, KC * INTER:2 * KC * INTER].rearrange("p (k i) -> p k i", k=KC)
    w_down = ffn_w[:, 2 * KC * INTER:FFN_W].rearrange("p (c h) -> p c h", c=IC)
    with ExitStack() as ctx:
        def sb(name, shape, dt):
            return ctx.enter_context(nc.sbuf_tensor(name, shape, dt))

        def sem(name):
            return ctx.enter_context(nc.semaphore(name))

        stats = sb("stats2", [P, TILES, 6], F32)
        meanvar = sb("meanvar2", [P, TILES, 2], F32)
        work = sb("work2", [P, 4, TILES], F32)
        rstd = sb("rstd2", [P, TILES], F32)
        ag = sb("ag", [P, IC], F32)
        au = sb("au", [P, IC], F32)
        ad = sb("ad", [P, HID], F32)
        gate = sb("gate", [P, 2, 512], F32)
        h32 = sb("h32", [P, 2, 512], F32)
        hh = sb("hh", [P, 2, 512], F16)
        hl = sb("hl", [P, 2, 512], F16)
        y = sb("y", [P, 2, HID], F32)
        staged = sb("staged", [P, 2, HID], F32)

        banks = [ctx.enter_context(nc.psum_tensor(f"ps_c{i}", [P, 512], F32)) for i in range(8)]
        ps_g, ps_u, ps_d = banks[0:2], banks[2:4], banks[4:8]

        stat, root = sem("stat2"), sem("root2")
        small_in = sem("small_in")
        x2_ready, x2_t, x2h_ready, x2l_ready = sem("x2_ready"), sem("x2_t"), sem("x2h_ready"), sem("x2l_ready")
        gu_done, gate_ready, h32_ready, hh_ready, hl_ready = (
            sem("gu_done"), sem("gate_ready"), sem("h32_ready"), sem("hh_ready"), sem("hl_ready"))
        down_done, y_ready, y_added = sem("down_done"), sem("y_ready"), sem("y_added")
        x3_ready, out_sent = sem("x3_ready"), sem("out_sent")
        block = ctx.enter_context(nc.Block())

        def rows(ic):
            return P if ic < IC - 1 else ILAST

        @block.sync
        def _(sp):
            for v, src in ((ag, ag_d), (au, au_d)):
                with nc.allow_non_contiguous_dma("one column per chunk"):
                    sp.dma_start(v[:, 0:IC - 1], src[0:(IC - 1) * P].rearrange("(c p) -> p c", p=P)
                                 ).then_inc(small_in, 16)
                    sp.dma_start(v[0:ILAST, IC - 1:IC], src[(IC - 1) * P:INTER].rearrange("(p c) -> p c", c=1)
                                 ).then_inc(small_in, 16)
            sp.dma_start(ad[:], ad_d.rearrange("(a f) -> a f", a=1).to_broadcast([P, HID])).then_inc(small_in, 16)
            with sp.Fori(0, TILES, 1) as t:
                sp.wait_ge(x3_ready, t + 1)
                sp.dma_start(out_d[bass.ds(t, 1), :, :].rearrange("a p f -> p (a f)"),
                             acc[:, bass.ds(t, 1), :].rearrange("p a f -> p (a f)")).then_inc(out_sent, 16)
            sp.wait_ge(out_sent, 16 * TILES)

        @block.scalar
        def _(act):
            act.wait_ge(stat, 2 * TILES + 1)
            nc.scalar.activation(work[:, 1, :], work[:, 0, :], ACT.Sqrt).then_inc(root, 1)

            def high(t, j):
                act.wait_ge(x2_t, t + 1)
                nc.scalar.activation(xth[:, :, bass.ds(t * P, P)], ps_g[j][:].rearrange("p (k c) -> p k c", k=KC),
                                     ACT.Copy).then_inc(x2h_ready, 1)

            with act.Fori(0, last(TILES, 2), 2) as t:
                high(t, 0)
                high(t + 1, 1)

            act.wait_ge(small_in, 80)
            with act.Fori(0, GROUPS, 1) as g:
                for ic in range(IC):
                    r, par = rows(ic), ic % 2
                    u = g * IC + ic
                    act.wait_ge(gu_done, u + 1)
                    nc.scalar.activation(gate[0:r, par, :], ps_g[par][0:r, :], ACT.Silu,
                                         scale=ag[0:r, ic:ic + 1]).then_inc(gate_ready, 1)
                    act.wait_ge(h32_ready, u + 1)
                    nc.scalar.activation(hh[0:r, par, :], h32[0:r, par, :], ACT.Copy).then_inc(hh_ready, 1)
            act.wait_ge(stat, 4 * TILES + 7)
            nc.scalar.activation(work[:, 1, :], work[:, 0, :], ACT.Sqrt).then_inc(root, 1)

        @block.vector
        def _(dve):
            n = norm_statistics(nc, dve, None, acc, stats, meanvar, rstd, work, stat, 0)
            dve.wait_ge(root, 1)
            n = norm_rstd(nc, dve, rstd, work, stat, n)

            def norm(t):
                tile = acc[:, bass.ds(t, 1), :].rearrange("p a f -> p (a f)")
                return normalise(nc, tile, tile, meanvar, rstd, t)

            def low(t, j):
                if above(t, t - 1):
                    dve.wait_ge(x2_t, t - 1)
                tile = acc[:, bass.ds(t, 1), :].rearrange("p a f -> p (a f)")
                normalise(nc, staged[:, j, :], tile, meanvar, rstd, t)
                norm(t).then_inc(x2_ready, 1)
                dve.wait_ge(x2h_ready, t + 1)
                nc.vector.tensor_tensor(xtl[:, :, bass.ds(t * P, P)], ps_g[j][:].rearrange("p (k c) -> p k c", k=KC),
                                        xth[:, :, bass.ds(t * P, P)], ALU.subtract).then_inc(x2l_ready, 1)

            low(0, 0)
            low(1, 1)
            with dve.Fori(2, last(TILES, 2), 2) as t:
                low(t, 0)
                low(t + 1, 1)

            dve.wait_ge(small_in, 80)
            with dve.Fori(0, GROUPS, 1) as g:
                for ic in range(IC):
                    r, par = rows(ic), ic % 2
                    u = g * IC + ic
                    dve.wait_ge(gate_ready, u + 1)
                    nc.vector.scalar_tensor_tensor(h32[0:r, par, :], ps_u[par][0:r, :], au[0:r, ic:ic + 1],
                                                   gate[0:r, par, :], ALU.mult, ALU.mult).then_inc(h32_ready, 1)
                    dve.wait_ge(hh_ready, u + 1)
                    nc.vector.tensor_tensor(hl[0:r, par, :], h32[0:r, par, :], hh[0:r, par, :],
                                            ALU.subtract).then_inc(hl_ready, 1)
                dve.wait_ge(down_done, g + 1)
                for tt in range(GT):
                    t = g * GT + tt
                    nc.vector.tensor_tensor(y[:, tt % 2, :], ps_d[tt][:], ad[:], ALU.mult).then_inc(y_ready, 1)
                    dve.wait_ge(y_ready, t + 1)
                    tile = acc[:, bass.ds(t, 1), :].rearrange("p a f -> p (a f)")
                    nc.vector.tensor_tensor(tile, y[:, tt % 2, :], tile, ALU.add).then_inc(y_added, 1)
            dve.wait_ge(y_added, TILES)
            n = norm_statistics(nc, dve, None, acc, stats, meanvar, rstd, work, stat, n)
            dve.wait_ge(root, 2)
            n = norm_rstd(nc, dve, rstd, work, stat, n)
            with dve.Fori(0, TILES, 1) as t:
                norm(t).then_inc(x3_ready, 1)

        @block.tensor
        def _(pe):
            def transpose(t, j):
                pe.wait_ge(x2_ready, t + 1)
                if above(t, t - 1):
                    pe.wait_ge(x2l_ready, t - 1)
                for k in range(KC):
                    m = nc.tensor.transpose(ps_g[j][:, k * P:(k + 1) * P],
                                            staged[:, j, k * P:(k + 1) * P], ident[:])
                m.then_inc(x2_t, 1)

            transpose(0, 0)
            transpose(1, 1)
            with pe.Fori(2, last(TILES, 2), 2) as t:
                transpose(t, 0)
                transpose(t + 1, 1)
            pe.wait_ge(x2l_ready, TILES)

            def down(g, ic):
                r, par = rows(ic), ic % 2
                pe.wait_ge(hl_ready, g * IC + ic + 1)
                for tt in range(GT):
                    c = slice(tt * P, (tt + 1) * P)
                    nc.tensor.matmul(ps_d[tt][:], hh[0:r, par, c], w_down[0:r, ic, :], start=(ic == 0), stop=False)
                    m = nc.tensor.matmul(ps_d[tt][:], hl[0:r, par, c], w_down[0:r, ic, :], start=False,
                                         stop=(ic == IC - 1))
                if ic == IC - 1:
                    m.then_inc(down_done, 1)

            def group(g):
                for ic in range(IC):
                    r, par = rows(ic), ic % 2
                    c = slice(ic * P, ic * P + r)
                    free = g * IC + ic - 1 if ic >= 2 else g * IC
                    if above(g, free):
                        pe.wait_ge(h32_ready, free)
                    for out, w in ((ps_g, w_gate), (ps_u, w_up)):
                        for k in range(KC):
                            nc.tensor.matmul(out[par][0:r, :], w[:, k, c], xth[:, k, bass.ds(g * 512, 512)],
                                             start=(k == 0), stop=False)
                            m = nc.tensor.matmul(out[par][0:r, :], w[:, k, c], xtl[:, k, bass.ds(g * 512, 512)],
                                                 start=False, stop=(k == KC - 1))
                    m.then_inc(gu_done, 1)
                    if ic == 1 and above(g, GT * g):
                        pe.wait_ge(y_added, GT * g)
                    if ic >= 1:
                        down(g, ic - 1)
                down(g, IC - 1)

            group(0)
            with pe.Fori(1, GROUPS, 1) as g:
                group(g)


def decoder_layer(nc, x_nat, x_t, ctx_nat, ctx_t, w_codes, w_scales, ffn_d, ag_d, au_d, ad_d,
                  cos_d, sin_d, mask_d, ident_d, out_d):
    with ExitStack() as ctx:
        def sb(name, shape, dt):
            return ctx.enter_context(nc.sbuf_tensor(name, shape, dt))

        keep = {
            "acc": sb("acc", [P, TILES, HID], F32),
            "xth": sb("xth", [P, KC, TOK], F16),
            "xtl": sb("xtl", [P, KC, TOK], F16),
            "ffn_w": sb("ffn_w", [P, FCH * CHUNK], F16),
            "ident": sb("ident", [P, P], F32),
        }
        attention(nc, keep, x_nat, x_t, w_codes, w_scales, cos_d, sin_d, mask_d, ident_d, ffn_d)
        cross_attention(nc, keep, ctx_nat, ctx_t)
        feed_forward(nc, keep, ag_d, au_d, ad_d, out_d)


def rotary_tables():
    pos = (np.arange(P) % SEQ).astype(np.float32)
    inv_freq = (1.0 / 10000.0 ** (np.arange(0, HD, 2, dtype=np.float32) / np.float32(HD))).astype(np.float32)
    f = pos[:, None] * inv_freq[None, :]
    c = np.repeat(np.cos(f.astype(np.float64)), 2, axis=1)
    s = np.stack([-np.sin(f.astype(np.float64)), np.sin(f.astype(np.float64))], axis=-1).reshape(P, HD)
    scale = np.array([HD ** -0.5] * REP + [1.0]) / WSCALE
    return ((scale[None, :, None] * c[:, None, :]).reshape(P, ROT).astype(np.float32),
            (scale[None, :, None] * s[:, None, :]).reshape(P, ROT).astype(np.float32))


def block_causal_mask():
    q, k = np.arange(P)[:, None], np.arange(P)[None, :]
    return np.where((q // SEQ == k // SEQ) & (k <= q), 0.0, -1e30).astype(np.float32)


def pack_group(q, k, v, o):
    parts = [q.reshape(KC, -1, NKV, REP * HD), k.reshape(KC, -1, NKV, HD), v.reshape(KC, -1, NKV, HD)]
    qkv = np.concatenate(parts, axis=3).transpose(2, 1, 0, 3)
    rows = o.reshape(NKV, REP, -1, HID).transpose(0, 2, 1, 3)
    n = qkv.shape[1]
    return np.concatenate([qkv.reshape(NKV, n, -1), rows.reshape(NKV, n, -1)], axis=2)


def by_chunk(a):
    g, n, w = a.shape
    return np.ascontiguousarray(a.reshape(g, n, w // CHUNK, CHUNK).transpose(0, 2, 1, 3).reshape(-1, n, CHUNK))


def pack_ffn(wg, wu, wd):
    down = np.zeros((IC * P, HID), np.float32)
    down[:INTER] = wd.T
    cols = np.concatenate([wg.T.reshape(KC, P, INTER).transpose(1, 0, 2).reshape(P, -1),
                           wu.T.reshape(KC, P, INTER).transpose(1, 0, 2).reshape(P, -1),
                           down.reshape(IC, P, HID).transpose(1, 0, 2).reshape(P, -1),
                           np.zeros((P, FCH * CHUNK - FFN_W), np.float32)], axis=1)
    return by_chunk(cols[None])


def kernel(x, ctx_4096, L0_attn_q_codes, L0_attn_q_scales, L0_attn_k_codes, L0_attn_k_scales,
           L0_attn_v_codes, L0_attn_v_scales, L0_attn_o_codes, L0_attn_o_scales, L0_ffn_Wg, L0_ffn_Wu,
           L0_ffn_Wd, L0_ffn_ag, L0_ffn_au, L0_ffn_ad):
    import concourse.bacc as bacc
    from concourse.bass_utils import run_bass_kernel_spmd

    a = [np.asarray(v) for v in (L0_attn_q_codes, L0_attn_k_codes, L0_attn_v_codes, L0_attn_o_codes)]
    s = [np.asarray(v) for v in (L0_attn_q_scales, L0_attn_k_scales, L0_attn_v_scales, L0_attn_o_scales)]
    x, c = np.asarray(x).reshape(TOK, HID), np.asarray(ctx_4096).reshape(TOK, HID)
    cos, sin = rotary_tables()
    host = {
        "x_nat": x.reshape(TILES, P, HID),
        "x_t": x.T.reshape(KC, P, TOK),
        "ctx_nat": c.reshape(TILES, P, HID),
        "ctx_t": c.T.reshape(KC, P, TOK),
        "w_codes": by_chunk(pack_group(*a)),
        "w_scales": by_chunk(pack_group(*s)).reshape(-1, CHUNK),
        "ffn_d": pack_ffn(np.asarray(L0_ffn_Wg), np.asarray(L0_ffn_Wu), np.asarray(L0_ffn_Wd)),
        "ag_d": np.asarray(L0_ffn_ag), "au_d": np.asarray(L0_ffn_au), "ad_d": np.asarray(L0_ffn_ad),
        "cos_d": cos, "sin_d": sin, "mask_d": block_causal_mask(), "ident_d": np.eye(P, dtype=np.float32),
    }
    nc = bacc.Bacc("TRN2", target_bir_lowering=False, num_devices=1)
    arrays, args = {}, {}
    for name, v in host.items():
        v = np.ascontiguousarray(v)
        arrays[f"in_{name}"] = v
        args[name] = nc.dram_tensor(f"in_{name}", v.shape, mybir.dt.from_np(v.dtype), kind="ExternalInput").ap()
    args["out_d"] = nc.dram_tensor("out_0", (TILES, P, HID), F32, kind="ExternalOutput").ap()
    decoder_layer(nc, **args)
    r = run_bass_kernel_spmd(nc, [arrays], core_ids=[0])
    return r.results[0]["out_0"].reshape(BATCH, SEQ, HID)
```

```python
import numpy as np
from contextlib import ExitStack

import concourse.bass as bass
from concourse import mybir

F32 = mybir.dt.float32
F16 = mybir.dt.float16
BF16 = mybir.dt.bfloat16
I32 = mybir.dt.int32
ALU = mybir.AluOpType
ACT = mybir.ActivationFunctionType
AX = mybir.AxisListType

P = 128
BATCH, SEQ, HID = 32, 64, 512
NH, NKV, HD = 32, 8, 128
REP = NH // NKV
TOK = BATCH * SEQ
TILES = TOK // P
KC = HID // P
QKV = (REP + 2) * HD
ROT = (REP + 1) * HD
GROUP_W = KC * QKV + REP * HID
CHUNK = 640
NCHUNK = GROUP_W // CHUNK
UNITS = NKV * TILES
STEP = 4
XB = STEP * P
INTER = 1376
IC = -(-INTER // P)
ILAST = INTER - (IC - 1) * P
FFN_W = 2 * KC * INTER + IC * HID
FCH = UNITS // STEP - TILES // STEP
WSCALE = 64.0
EPS = 1e-5


def in_range(n, lo, hi):
    return not isinstance(n, int) or lo <= n < hi


def last(end, step):
    return end - step + 1


def above(n, count):
    return not isinstance(n, int) or count > 0


def attention(nc, keep, x_nat, x_t, w_codes, w_scales, cos_d, sin_d, mask_d, ident_d, ffn_d):
    acc, xth, xtl, ffn_w, ident = keep["acc"], keep["xth"], keep["xtl"], keep["ffn_w"], keep["ident"]
    with ExitStack() as ctx:
        def sb(name, shape, dt):
            return ctx.enter_context(nc.sbuf_tensor(name, shape, dt))

        def pb(name, cols):
            return ctx.enter_context(nc.psum_tensor(name, [P, cols], F32))

        def sem(name):
            return ctx.enter_context(nc.semaphore(name))

        wh = sb("wh", [P, 2 * GROUP_W], F16)
        wl = sb("wl", [P, 2 * GROUP_W], F16)
        codes = sb("codes", [P, 2, CHUNK], I32)
        scales = sb("scales", [P, 2, CHUNK], F32)
        w32 = sb("w32", [P, 2, CHUNK], F32)
        ffn32 = sb("ffn32", [P, CHUNK], F32)
        xt32 = sb("xt32", [P, 2, KC, XB], F32)
        cos = sb("cos", [P, ROT], F32)
        sin = sb("sin", [P, ROT], F32)
        mask32 = sb("mask32", [P, SEQ], F32)
        mask = sb("mask", [P, REP * SEQ], BF16)
        identb = sb("identb", [P, P], BF16)
        rot_c = sb("rot_c", [P, ROT], F32)
        rot_s = sb("rot_s", [P, ROT], F32)
        rot = sb("rot", [P, ROT], F32)
        qkh = sb("qkh", [P, ROT], F16)
        qkl = sb("qkl", [P, ROT], F16)
        vh = sb("vh", [P, 2, HD], F16)
        vl = sb("vl", [P, 2, HD], F16)
        negmax = sb("negmax", [P, 2, REP], F32)
        sums = sb("sums", [P, 2, REP], F32)
        inv = sb("inv", [P, 2, REP], F32)
        prob = sb("prob", [P, REP, SEQ], F32)
        probn = sb("probn", [P, REP, SEQ], F32)
        pth = sb("pth", [P, REP * SEQ], F16)
        ptl = sb("ptl", [P, REP * SEQ], F16)
        oth = sb("oth", [P, 2, REP * P], F16)
        otl = sb("otl", [P, 2, REP * P], F16)

        ps_qkv = pb("ps_qkv", 1024)
        ps_qk = pb("ps_qk", 1024)
        ps_sp = pb("ps_sp", 512)
        ps_s, ps_p = ps_sp[:, 0:REP * SEQ], ps_sp[:, REP * SEQ:2 * REP * SEQ]
        ps_o = pb("ps_o", 1024)
        ps_o_view = ps_o[:].rearrange("p (b r) -> p b r", b=2)[:, :, 0:REP * SEQ].rearrange(
            "p b (h q) -> p b h q", h=REP)
        ps_out = pb("ps_out", 512)

        const_in = sem("const_in")
        xt_in = [sem("xt_in0"), sem("xt_in1")]
        x_in = sem("x_in")
        chunk_in = [sem("chunk_in0"), sem("chunk_in1")]
        ffn_in = sem("ffn_in")
        consts = sem("consts")
        xth_ready, xtl_ready = sem("xth_ready"), sem("xtl_ready")
        w32_ready, wh_ready, wl_ready = sem("w32_ready"), sem("wh_ready"), sem("wl_ready")
        ffn_ready = sem("ffn_ready")
        qkv_done, qk_t, scores, p_t, pv_done, out_done = (
            sem("qkv_done"), sem("qk_t"), sem("scores"), sem("p_t"), sem("pv_done"), sem("out_done"))
        rot_parts, rotated = sem("rot_parts"), sem("rotated")
        qkh_ready, qkl_ready = sem("qkh_ready"), sem("qkl_ready")
        vh_ready, vl_ready = sem("vh_ready"), sem("vl_ready")
        max_ready, exp_ready, inv_ready, prob_ready = (
            sem("max_ready"), sem("exp_ready"), sem("inv_ready"), sem("prob_ready"))
        pth_ready, ptl_ready = sem("pth_ready"), sem("ptl_ready")
        oth_ready, otl_ready = sem("oth_ready"), sem("otl_ready")
        acc_added = sem("acc_added")

        def wcol(n, at):
            return (n // TILES) % 2 * GROUP_W + at

        def by_sequence(tile):
            return tile.rearrange("p (h b q) -> p b h q", h=REP, b=2)

        def xcol(n):
            return n % TILES * P

        block = ctx.enter_context(nc.Block())

        @block.sync
        def _(sp):
            def load_chunk(c, buf):
                if above(c, c - 1):
                    sp.wait_ge(w32_ready, c - 1)
                sp.dma_start(codes[:, buf, :], w_codes[bass.ds(c, 1), :, :].rearrange("a p f -> p (a f)")
                             ).then_inc(chunk_in[buf], 16)
                sp.dma_start(scales[:, buf, :], w_scales[bass.ds(c, 1), :].to_broadcast([P, CHUNK])
                             ).then_inc(chunk_in[buf], 16)

            load_chunk(0, 0)
            load_chunk(1, 1)
            for dst, src in ((cos, cos_d), (sin, sin_d), (mask32, mask_d), (ident, ident_d)):
                sp.dma_start(dst[:], src).then_inc(const_in, 16)
            sp.dma_start(acc[:], x_nat.rearrange("t p f -> p t f")).then_inc(x_in, 16)
            with sp.Fori(2, last(NKV * NCHUNK, 2), 2) as c:
                load_chunk(c, 0)
                load_chunk(c + 1, 1)

        @block.gpsimd
        def _(pool):
            def load_x(i):
                if i >= 2:
                    pool.wait_ge(xtl_ready, i - 1)
                pool.dma_start(xt32[:, i % 2], x_t[:, :, i * XB:(i + 1) * XB].rearrange("k p c -> p k c")
                               ).then_inc(xt_in[i % 2], 16)

            load_x(0)
            load_x(1)

            def slot(n, par, load_ffn):
                if load_ffn is not None:
                    if above(n, load_ffn):
                        pool.wait_ge(ffn_ready, load_ffn)
                    pool.dma_start(ffn32[:], ffn_d[bass.ds(load_ffn, 1), :, :].rearrange("a p f -> p (a f)")
                                   ).then_inc(ffn_in, 16)
                if in_range(n, 1, UNITS + 1):
                    pool.wait_ge(inv_ready, n)
                    if above(n, n - 1):
                        pool.wait_ge(p_t, n - 1)
                    nc.gpsimd.tensor_tensor(
                        probn[:], prob[:],
                        inv[:, 1 - par, :].unsqueeze(2).to_broadcast([P, REP, SEQ]),
                        ALU.mult).then_inc(prob_ready, 1)
                if in_range(n, 0, UNITS):
                    pool.wait_ge(rot_parts, 2 * n + 2)
                    if above(n, n):
                        pool.wait_ge(qk_t, n)
                    nc.gpsimd.tensor_tensor(rot[:], rot_c[:], rot_s[:], ALU.add).then_inc(rotated, 1)

            def body(n0, ffn):
                for j in range(STEP):
                    slot(n0 + j, j % 2, n0 // STEP if ffn and j == 0 else None)

            for j in range(STEP):
                slot(j, j % 2, 0 if j == 0 else None)
                if j + 2 < TOK // XB:
                    load_x(j + 2)
            with pool.Fori(STEP, last(UNITS - TILES, STEP), STEP) as n0:
                body(n0, True)
            with pool.Fori(UNITS - TILES, last(UNITS, STEP), STEP) as n0:
                body(n0, False)
            slot(UNITS, 0, None)

        @block.scalar
        def _(act):
            act.wait_ge(const_in, 64)
            nc.scalar.activation(identb[:], ident[:], ACT.Copy)
            nc.scalar.activation(mask[:].rearrange("p (h k) -> p h k", h=REP),
                                 mask32[:].unsqueeze(1).to_broadcast([P, REP, SEQ]), ACT.Copy).then_inc(consts, 1)

            def chunk_high(c, buf):
                act.wait_ge(w32_ready, c + 1)
                nc.scalar.activation(wh[:, bass.ds(c % (2 * NCHUNK) * CHUNK, CHUNK)], w32[:, buf, :],
                                     ACT.Copy, scale=WSCALE).then_inc(wh_ready, 1)

            def x_high(i):
                act.wait_ge(xt_in[i % 2], 16 * (i // 2 + 1))
                nc.scalar.activation(xth[:, :, i * XB:(i + 1) * XB], xt32[:, i % 2], ACT.Copy).then_inc(xth_ready, 1)

            for c in range(NCHUNK):
                chunk_high(c, c % 2)
                if c == 0:
                    x_high(0)

            def slot(n, par, chunk, buf):
                if in_range(n, 1, UNITS + 1):
                    act.wait_ge(qk_t, n)
                    nc.scalar.activation(qkh[:], ps_qk[:, 0:ROT], ACT.Copy).then_inc(qkh_ready, 1)
                    act.wait_ge(max_ready, n)
                    if above(n, n - 1):
                        act.wait_ge(prob_ready, n - 1)
                    for h in range(REP):
                        e = nc.scalar.activation(prob[:, h, :], ps_s[:, h * SEQ:(h + 1) * SEQ], ACT.Exp,
                                                 bias=negmax[:, 1 - par, h:h + 1],
                                                 accum_out=sums[:, 1 - par, h:h + 1])
                    e.then_inc(exp_ready, 1)
                if chunk is not None:
                    chunk_high(chunk, buf)
                if in_range(n, 1, UNITS + 1):
                    act.wait_ge(p_t, n)
                    if above(n, n - 1):
                        act.wait_ge(pv_done, n - 1)
                    nc.scalar.activation(pth[:], ps_p, ACT.Copy).then_inc(pth_ready, 1)
                if in_range(n, 0, UNITS):
                    act.wait_ge(rot_parts, 2 * n + 2)
                    if above(n, n - 1):
                        act.wait_ge(pv_done, n - 1)
                    nc.scalar.activation(vh[:, par, :], ps_qkv[:, ROT:QKV], ACT.Copy,
                                         scale=1.0 / WSCALE).then_inc(vh_ready, 1)
                if in_range(n, 1, UNITS + 1):
                    act.wait_ge(pv_done, n)
                    nc.scalar.activation(by_sequence(oth[:, 1 - par, :]), ps_o_view, ACT.Copy).then_inc(oth_ready, 1)

            def body(n0, chunks, x_blocks=0):
                for j in range(STEP):
                    slot(n0 + j, j % 2, n0 // 2 + NCHUNK + j // 2 if chunks and j % 2 == 0 else None, j // 2)
                    if j + 1 < x_blocks:
                        x_high(j + 1)
                    if chunks and j == 3:
                        act.wait_ge(ffn_in, n0 // STEP * 16 + 16)
                        nc.scalar.activation(ffn_w[:, bass.ds(n0 // STEP * CHUNK, CHUNK)], ffn32[:],
                                             ACT.Copy).then_inc(ffn_ready, 1)

            body(0, True, TOK // XB)
            with act.Fori(STEP, last(UNITS - TILES, STEP), STEP) as n0:
                body(n0, True)
            with act.Fori(UNITS - TILES, last(UNITS, STEP), STEP) as n0:
                body(n0, False)
            slot(UNITS, 0, None, 0)

        @block.vector
        def _(dve):
            def dequantise(c, buf):
                dve.wait_ge(chunk_in[buf], c // 2 * 32 + 32)
                if above(c, c - 1):
                    dve.wait_ge(wh_ready, c - 1)
                    dve.wait_ge(wl_ready, c - 1)
                nc.vector.scalar_tensor_tensor(w32[:, buf, :], codes[:, buf, :], -8.0, scales[:, buf, :],
                                               ALU.add, ALU.mult).then_inc(w32_ready, 1)

            def chunk_low(c, buf):
                dve.wait_ge(wh_ready, c + 1)
                at = bass.ds(c % (2 * NCHUNK) * CHUNK, CHUNK)
                nc.vector.scalar_tensor_tensor(wl[:, at], w32[:, buf, :], WSCALE, wh[:, at],
                                               ALU.mult, ALU.subtract).then_inc(wl_ready, 1)

            def x_low(i):
                dve.wait_ge(xth_ready, i + 1)
                at = slice(i * XB, (i + 1) * XB)
                nc.vector.tensor_tensor(xtl[:, :, at], xt32[:, i % 2], xth[:, :, at],
                                        ALU.subtract).then_inc(xtl_ready, 1)

            dequantise(0, 0)
            for c in range(NCHUNK):
                if c + 1 < NCHUNK:
                    dequantise(c + 1, (c + 1) % 2)
                chunk_low(c, c % 2)
                if c == 0:
                    x_low(0)
            def slot(n, par, chunk, buf, final=False):
                if in_range(n, 1, UNITS + 1):
                    dve.wait_ge(qkh_ready, n)
                    nc.vector.tensor_tensor(qkl[:], ps_qk[:, 0:ROT], qkh[:], ALU.subtract).then_inc(qkl_ready, 1)
                if in_range(n, 3, UNITS + 3):
                    dve.wait_ge(out_done, n - 2)
                    if isinstance(n, int) and n == 3:
                        dve.wait_ge(x_in, 16)
                    if above(n, n - 3):
                        dve.wait_ge(acc_added, n - 3)
                    tile = acc[:, bass.ds((n + 2 * TILES - 3) % TILES, 1), :].rearrange("p a f -> p (a f)")
                    nc.vector.scalar_tensor_tensor(tile, ps_out[:], 1.0 / WSCALE, tile,
                                                   ALU.mult, ALU.add).then_inc(acc_added, 1)
                if in_range(n, 1, UNITS + 1):
                    dve.wait_ge(scores, n)
                    nc.vector.tensor_reduce(negmax[:, 1 - par, :], ps_s.rearrange("p (h k) -> p h k", h=REP),
                                            AX.X, ALU.max, negate=True).then_inc(max_ready, 1)
                if chunk is not None:
                    if above(n, n):
                        dve.wait_ge(qkv_done, n)
                    if above(n, n - 2):
                        dve.wait_ge(out_done, n - 2)
                    dequantise(chunk, buf)
                if final:
                    dve.wait_ge(acc_added, n - 2)
                if in_range(n, 1, UNITS + 1):
                    dve.wait_ge(exp_ready, n)
                    nc.vector.reciprocal(inv[:, 1 - par, :], sums[:, 1 - par, :]).then_inc(inv_ready, 1)
                if final:
                    tile_statistics(nc, acc, keep["stats"], (n + 2 * TILES - 3) % TILES)
                if in_range(n, 0, UNITS):
                    dve.wait_ge(qkv_done, n + 1)
                    if above(n, n):
                        dve.wait_ge(rotated, n)
                    nc.vector.tensor_tensor(rot_c[:], ps_qkv[:, 0:ROT], cos[:], ALU.mult).then_inc(rot_parts, 1)
                    src = ps_qkv[:, 0:ROT].rearrange("p (i two) -> p two i", two=2)
                    dst = rot_s[:].rearrange("p (i two) -> p two i", two=2)
                    tab = sin[:].rearrange("p (i two) -> p two i", two=2)
                    nc.vector.tensor_tensor(dst, src[:, ::-1, :], tab, ALU.mult).then_inc(rot_parts, 1)
                if in_range(n, 1, UNITS + 1):
                    dve.wait_ge(pth_ready, n)
                    nc.vector.tensor_tensor(ptl[:], ps_p, pth[:], ALU.subtract).then_inc(ptl_ready, 1)
                if in_range(n, 0, UNITS):
                    dve.wait_ge(vh_ready, n + 1)
                    if above(n, n - 1):
                        dve.wait_ge(pv_done, n - 1)
                    nc.vector.scalar_tensor_tensor(vl[:, par, :], ps_qkv[:, ROT:QKV], 1.0 / WSCALE,
                                                   vh[:, par, :], ALU.mult, ALU.subtract).then_inc(vl_ready, 1)
                if chunk is not None:
                    chunk_low(chunk, buf)
                if in_range(n, 1, UNITS + 1):
                    dve.wait_ge(oth_ready, n)
                    nc.vector.tensor_tensor(by_sequence(otl[:, 1 - par, :]), ps_o_view,
                                            by_sequence(oth[:, 1 - par, :]), ALU.subtract).then_inc(otl_ready, 1)

            def body(n0, chunks):
                for j in range(STEP):
                    slot(n0 + j, j % 2, n0 // 2 + NCHUNK + j // 2 if chunks and j % 2 == 0 else None, j // 2,
                         not chunks)

            for j in range(STEP):
                slot(j, j % 2, NCHUNK + j // 2 if j % 2 == 0 else None, j // 2)
                if j + 1 < TOK // XB:
                    x_low(j + 1)
            with dve.Fori(STEP, last(UNITS - TILES, STEP), STEP) as n0:
                body(n0, True)
            with dve.Fori(UNITS - TILES, last(UNITS, STEP), STEP) as n0:
                body(n0, False)
            for n in range(UNITS, UNITS + 3):
                slot(n, n % 2, None, 0, True)

        @block.tensor
        def _(pe):
            pe.wait_ge(consts, 1)

            def slot(n, par):
                first = isinstance(n, int) and n == 0

                def qkv(chunks):
                    for k in chunks:
                        if first:
                            pe.wait_ge(wl_ready, -(-(k + 1) * QKV // CHUNK))
                        for w_at, width, ps_at in ((0, 512, 0), (512, QKV - 512, 512)):
                            at = bass.ds(wcol(n, k * QKV + w_at), width)
                            out = ps_qkv[:, ps_at:ps_at + width]
                            xh = xth[:, k, bass.ds(xcol(n), P)]
                            xl = xtl[:, k, bass.ds(xcol(n), P)]
                            nc.tensor.matmul(out, xh, wh[:, at], start=(k == 0), stop=False)
                            nc.tensor.matmul(out, xh, wl[:, at], start=False, stop=False)
                            m = nc.tensor.matmul(out, xl, wh[:, at], start=False, stop=(k == KC - 1))
                    return m

                if in_range(n, 0, UNITS):
                    if first:
                        pe.wait_ge(xtl_ready, 1)
                    else:
                        pe.wait_ge(wl_ready, n // TILES * NCHUNK + NCHUNK)
                    if above(n, n):
                        pe.wait_ge(vl_ready, n)
                    qkv(range(KC // 2))
                if in_range(n, 1, UNITS + 1):
                    if above(n, n - 1):
                        pe.wait_ge(ptl_ready, n - 1)
                    nc.tensor.matmul(ps_s, identb[:], mask[:], start=True, stop=False)
                    parts = [(ps_s[:, i * SEQ:(i + 1) * SEQ], slice(i * P, (i + 1) * P),
                              slice(REP * P + i % 2 * SEQ, REP * P + (i % 2 + 1) * SEQ)) for i in range(REP)]
                    pe.wait_ge(qkh_ready, n)
                    for out, q, k in parts:
                        nc.tensor.matmul(out, qkh[:, q], qkh[:, k], start=False, stop=False)
                    pe.wait_ge(qkl_ready, n)
                    for i, (out, q, k) in enumerate(parts):
                        nc.tensor.matmul(out, qkh[:, q], qkl[:, k], start=False, stop=False)
                        m = nc.tensor.matmul(out, qkl[:, q], qkh[:, k], start=False, stop=(i == REP - 1))
                    m.then_inc(scores, 1)
                if in_range(n, 0, UNITS):
                    qkv(range(KC // 2, KC)).then_inc(qkv_done, 1)

                def project(h):
                    if not in_range(n, 2, UNITS + 2):
                        return
                    if h == 0:
                        pe.wait_ge(otl_ready, n - 1)
                        if above(n, n - 2):
                            pe.wait_ge(acc_added, n - 2)
                    w = bass.ds(wcol(n + 2 * TILES - 2, KC * QKV + h * HID), HID)
                    oh = oth[:, par, h * P:(h + 1) * P]
                    nc.tensor.matmul(ps_out[:], oh, wh[:, w], start=(h == 0), stop=False)
                    nc.tensor.matmul(ps_out[:], oh, wl[:, w], start=False, stop=False)
                    m = nc.tensor.matmul(ps_out[:], otl[:, par, h * P:(h + 1) * P], wh[:, w],
                                         start=False, stop=(h == REP - 1))
                    if h == REP - 1:
                        m.then_inc(out_done, 1)

                project(0)
                project(1)
                if in_range(n, 1, UNITS + 1):
                    pe.wait_ge(prob_ready, n)
                    if above(n, n - 1):
                        pe.wait_ge(ptl_ready, n - 1)
                    for pair in range(REP // 2):
                        m = nc.tensor.transpose(ps_p[:, pair * P:(pair + 1) * P], probn[:, 2 * pair:2 * pair + 2, :]
                                                .rearrange("p b k -> p (b k)"), ident[:])
                    m.then_inc(p_t, 1)

                project(2)
                project(3)
                if in_range(n, 1, UNITS + 1):
                    pe.wait_ge(pth_ready, n)
                    pe.wait_ge(vl_ready, n)
                    if above(n, n - 1):
                        pe.wait_ge(otl_ready, n - 1)
                    seqs = [(slice(b * SEQ, (b + 1) * SEQ), ps_o[:, 512 * b:512 * b + REP * SEQ]) for b in range(2)]
                    for v in (vh, vl):
                        for own, out in seqs:
                            nc.tensor.matmul(out, v[own, 1 - par, :], pth[own, :], start=(v is vh), stop=False)
                    pe.wait_ge(ptl_ready, n)
                    for own, out in seqs:
                        m = nc.tensor.matmul(out, vh[own, 1 - par, :], ptl[own, :], start=False, stop=True)
                    m.then_inc(pv_done, 1)
                if in_range(n, 0, UNITS):
                    pe.wait_ge(rotated, n + 1)
                    if above(n, n):
                        pe.wait_ge(qkl_ready, n)
                    for h in range(REP):
                        pair = ps_qk[:, h // 2 * 2 * P:(h // 2 + 1) * 2 * P]
                        nc.tensor.transpose(pair.rearrange("p (b h q) -> p h b q", b=2, h=2)[:, h % 2],
                                            rot[:, h * P:(h + 1) * P], ident[:])
                    nc.tensor.transpose(ps_qk[:, REP * P:ROT], rot[:, REP * P:ROT], ident[:]).then_inc(qk_t, 1)

            for n in range(STEP):
                slot(n, n % 2)
            pe.wait_ge(xtl_ready, TOK // XB)
            with pe.Fori(STEP, last(UNITS, STEP), STEP) as n0:
                for j in range(STEP):
                    slot(n0 + j, j % 2)
            for n in range(UNITS, UNITS + 2):
                slot(n, n % 2)


def tile_statistics(nc, acc, stats, t):
    return nc.vector.bn_stats(stats[:, bass.ds(t, 1), :].rearrange("p a f -> p (a f)"),
                              acc[:, bass.ds(t, 1), :].rearrange("p a f -> p (a f)"))


def norm_variance(nc, dve, stats, meanvar, work, sem_dve, count):
    n = work.shape[2]
    for t in range(n):
        nc.vector.bn_aggr(meanvar[:, t, :], stats[:, t, :]).then_inc(sem_dve, 1)
    dve.wait_ge(sem_dve, count + n)
    nc.vector.tensor_scalar(work[:, 0, :], meanvar[:, :, 1], EPS, None, ALU.add).then_inc(sem_dve, 1)
    return count + n + 1


def norm_rstd(nc, dve, rstd, work, sem_dve, count):
    def step(ins, n):
        ins.then_inc(sem_dve, 1)
        dve.wait_ge(sem_dve, n)

    v, root, r, a = (work[:, i, :] for i in range(4))
    step(nc.vector.reciprocal(r, root), count + 1)
    step(nc.vector.tensor_tensor(a, r, r, ALU.mult), count + 2)
    step(nc.vector.tensor_tensor(root, a, v, ALU.mult), count + 3)
    step(nc.vector.tensor_scalar(a, root, -0.5, 1.5, ALU.mult, ALU.add), count + 4)
    step(nc.vector.tensor_tensor(rstd[:], r, a, ALU.mult), count + 5)
    return count + 5


def normalise(nc, out, tile, meanvar, rstd, t):
    mean = meanvar[:, bass.ds(t, 1), 0:1].rearrange("p a f -> p (a f)")
    return nc.vector.tensor_scalar(out, tile, mean, rstd[:, bass.ds(t, 1)], ALU.subtract, ALU.mult)


def cross_attention(nc, keep, ctx_nat, ctx_t):
    acc, ident = keep["acc"], keep["ident"]
    SCALE = float(SEQ) ** -0.5
    VC = SEQ + 1
    FILLS = 7
    with ExitStack() as ctx:
        def sb(name, shape, dt):
            return ctx.enter_context(nc.sbuf_tensor(name, shape, dt))

        def pb(name, cols, dt=F32):
            return ctx.enter_context(nc.psum_tensor(name, [P, cols], dt))

        def sem(name):
            return ctx.enter_context(nc.semaphore(name))

        stats = keep["stats"]
        meanvar = sb("meanvar1", [P, TILES, 2], F32)
        work = sb("work1", [P, 4, TILES], F32)
        rstd = sb("rstd1", [P, TILES], F32)
        identh = sb("identh", [P, P], F16)
        ct32 = sb("ct32", [P, 2, TOK], F32)
        vth = sb("vth", [P, KC, BATCH, VC], F16)
        vtl = sb("vtl", [P, KC, BATCH, SEQ], F16)
        ctx32 = sb("ctx32", [P, 2, HID], F32)
        q_pair = sb("q_pair", [P, 4, HID], F16)
        k_pair = sb("k_pair", [P, 4, HID], F16)
        q_high = sb("q_high", [P, 4, HID], F16)
        k_low = sb("k_low", [P, 4, HID], F16)
        negmax = sb("negmax1", [P, 2, KC], F32)
        negmax_parts = sb("negmax_parts", [P, 2, KC, 2], F16)
        e32 = sb("e32", [P, 2, HID], F32)
        ph = sb("ph", [P, 2, KC, HID], F16)
        pl = sb("pl", [P, 2, KC, HID], F16)
        inv = sb("inv1", [P, 2, KC], F32)
        un = sb("un", [P, 2, KC, P], F32)

        ps_s = [pb("ps_smax0", HID), pb("ps_smax1", HID)]
        ps_e = [pb("ps_e0", HID), pb("ps_e1", HID)]
        ps_v = [pb("ps_v0", HID), pb("ps_v1", HID)]
        ps_n = pb("ps_n", 1024, F16)
        ps_x = pb("ps_x", HID)

        stat = sem("stat1")
        root = sem("root1")
        ct_in = [sem("ct_in0"), sem("ct_in1")]
        vth_ready, vtl_ready = sem("vth_ready"), sem("vtl_ready")
        ctx_in = [sem("ctx_in0"), sem("ctx_in1")]
        fills = sem("fills")
        ident_ready = sem("ident_ready")
        x1_ready = sem("x1_ready")
        high_ready, low_ready = sem("high_ready"), sem("low_ready")
        smax_done, max_ready, parts_ready, parts_t, row_ready = (
            sem("smax_done"), sem("max_ready1"), sem("parts_ready"), sem("parts_t"), sem("row_ready"))
        s_done, exp_ready, ph_ready, pl_ready = sem("s_done"), sem("exp_ready1"), sem("ph_ready"), sem("pl_ready")
        pv_done, inv_ready, un_ready, un_t, x_added = (
            sem("pv_done1"), sem("inv_ready1"), sem("un_ready"), sem("un_t"), sem("x_added"))

        def mine(b):
            return slice(0, SEQ) if b % 2 == 0 else slice(SEQ, P)

        def other(b):
            return slice(SEQ, P) if b % 2 == 0 else slice(0, SEQ)

        block = ctx.enter_context(nc.Block())

        def run(eng, slot, first, end):
            for s in range(first, 4):
                slot(s, s % 4)
            with eng.Fori(4, last(BATCH - 4, 4), 4) as s0:
                for j in range(4):
                    slot(s0 + j, j)
            for s in range(BATCH - 4, end):
                slot(s, s % 4)

        @block.sync
        def _(sp):
            def load_t(k):
                if k >= 2:
                    sp.wait_ge(vtl_ready, k - 1)
                sp.dma_start(ct32[:, k % 2, :], ctx_t[k, :, :]).then_inc(ct_in[k % 2], 16)

            def load(t, buf):
                if above(t, 2 * t - 2):
                    sp.wait_ge(low_ready, 2 * t - 2)
                sp.dma_start(ctx32[:, buf, :], ctx_nat[bass.ds(t, 1), :, :].rearrange("a p f -> p (a f)")
                             ).then_inc(ctx_in[buf], 16)

            load(0, 0)
            load(1, 1)
            for k in range(KC):
                load_t(k)
            with sp.Fori(2, last(TILES, 2), 2) as t:
                load(t, 0)
                load(t + 1, 1)

        @block.gpsimd
        def _(pool):
            filled = 0
            for what, value in [(q_high[:], 0.0), (k_low[:], 0.0), (vth[:, :, :, SEQ:VC], 1.0)] + [
                    (q_high[other(i).start:other(i).start + 2, i, :], 1.0) for i in range(4)]:
                if filled:
                    pool.wait_ge(fills, filled)
                nc.gpsimd.memset(what, value).then_inc(fills, 1)
                filled += 1

            def slot(s, j):
                if in_range(s, 2, BATCH + 2):
                    for mc in range(KC):
                        pool.wait_ge(ph_ready, (s - 2) * KC + mc + 1)
                        nc.gpsimd.tensor_tensor(pl[:, j % 2, mc, :], e32[:, mc % 2, :], ph[:, j % 2, mc, :],
                                                ALU.subtract).then_inc(pl_ready, 1)

            run(pool, slot, 0, BATCH + 2)

        @block.scalar
        def _(act):
            nc.scalar.activation(identh[:], ident[:], ACT.Copy).then_inc(ident_ready, 1)
            act.wait_ge(stat, TILES + 1)
            nc.scalar.activation(work[:, 1, :], work[:, 0, :], ACT.Sqrt).then_inc(root, 1)

            def prepare(b, j, part):
                if part == 0:
                    act.wait_ge(x1_ready, b // 2 + 1)
                    if above(b, KC * (b - 3)):
                        act.wait_ge(s_done, KC * (b - 3))
                    nc.scalar.activation(q_pair[mine(j), j, :], acc[mine(j), bass.ds(b // 2, 1), :]
                                         .rearrange("p a f -> p (a f)"), ACT.Copy).then_inc(high_ready, 1)
                else:
                    act.wait_ge(ctx_in[j // 2], b // 4 * 16 + 16)
                    nc.scalar.activation(k_pair[mine(j), j, :], ctx32[mine(j), j // 2, :],
                                         ACT.Copy).then_inc(high_ready, 1)

            def ctx_high(k):
                act.wait_ge(ct_in[k % 2], 16 * (k // 2 + 1))
                nc.scalar.activation(vth[:, k, :, 0:SEQ], ct32[:, k % 2, :].rearrange("p (b c) -> p b c", b=BATCH),
                                     ACT.Copy).then_inc(vth_ready, 1)

            prepare(0, 0, 0)
            prepare(0, 0, 1)

            def slot(s, j):
                for mc in range(KC):
                    if mc < 2 and in_range(s, 0, BATCH - 1):
                        prepare(s + 1, (j + 1) % 4, mc)
                    if in_range(s, 2, BATCH + 2):
                        c = (s - 2) * KC + mc
                        act.wait_ge(s_done, c + 1)
                        if above(c, c - 1):
                            act.wait_ge(pl_ready, c - 1)
                        nc.scalar.activation(e32[:, mc % 2, :], ps_e[mc % 2][:], ACT.Exp,
                                             scale=SCALE).then_inc(exp_ready, 1)
                        if mc == 0 and above(s, s - 3):
                            act.wait_ge(pv_done, s - 3)
                        act.wait_ge(exp_ready, c + 1)
                        nc.scalar.activation(ph[:, j % 2, mc, :], e32[:, mc % 2, :], ACT.Copy).then_inc(ph_ready, 1)
                if isinstance(s, int) and s < 2:
                    ctx_high(2 * s)
                    ctx_high(2 * s + 1)

            run(act, slot, 0, BATCH + 2)

        @block.vector
        def _(dve):
            done = norm_variance(nc, dve, stats, meanvar, work, stat, 0)
            dve.wait_ge(root, 1)
            norm_rstd(nc, dve, rstd, work, stat, done)

            def norm(t):
                tile = acc[:, bass.ds(t, 1), :].rearrange("p a f -> p (a f)")
                normalise(nc, tile, tile, meanvar, rstd, t).then_inc(x1_ready, 1)

            norm(0)
            norm(1)
            dve.wait_ge(fills, FILLS)

            def prepare(b, j, part):
                if part == 0:
                    dve.wait_ge(high_ready, 2 * b + 1)
                    dve.wait_ge(x1_ready, b // 2 + 1)
                    nc.vector.tensor_tensor(q_pair[other(j), j, :], acc[mine(j), bass.ds(b // 2, 1), :]
                                            .rearrange("p a f -> p (a f)"), q_pair[mine(j), j, :], ALU.subtract)
                elif part == 1:
                    nc.vector.tensor_copy(q_high[mine(j), j, :], q_pair[mine(j), j, :])
                    dve.wait_ge(high_ready, 2 * b + 2)
                    nc.vector.tensor_copy(k_pair[other(j), j, :], k_pair[mine(j), j, :])
                else:
                    nc.vector.tensor_tensor(k_low[mine(j), j, :], ctx32[mine(j), j // 2, :],
                                            k_pair[mine(j), j, :], ALU.subtract).then_inc(low_ready, 1)

            def ctx_low(k):
                dve.wait_ge(vth_ready, k + 1)
                nc.vector.tensor_tensor(vtl[:, k, :, :], ct32[:, k % 2, :].rearrange("p (b c) -> p b c", b=BATCH),
                                        vth[:, k, :, 0:SEQ], ALU.subtract).then_inc(vtl_ready, 1)

            for part in range(3):
                prepare(0, 0, part)

            def slot(s, j):
                if in_range(s, 1, BATCH + 1):
                    dve.wait_ge(parts_t, s)
                    b1 = (j - 1) % 4
                    at = other(b1).start
                    nc.vector.tensor_copy(k_low[at:at + 2, b1, :], ps_n[0:2, 0:HID]).then_inc(row_ready, 1)
                if j % 2 == 1 and in_range(s, 0, BATCH - 4):
                    norm((s + 3) // 2)
                for mc in range(KC):
                    if in_range(s, 0, BATCH):
                        dve.wait_ge(smax_done, s * KC + mc + 1)
                        nc.vector.tensor_reduce(negmax[:, j % 2, mc:mc + 1], ps_s[mc % 2][:], AX.X, ALU.max,
                                                negate=True).then_inc(max_ready, 1)
                    if mc > 0 and in_range(s, 0, BATCH - 1):
                        prepare(s + 1, (j + 1) % 4, mc - 1)
                if isinstance(s, int) and s < 2:
                    ctx_low(2 * s)
                    ctx_low(2 * s + 1)
                if in_range(s, 0, BATCH):
                    dve.wait_ge(max_ready, KC * (s + 1))
                    if above(s, s - 1):
                        dve.wait_ge(parts_t, s - 1)
                    nc.vector.tensor_copy(negmax_parts[:, j % 2, :, 0], negmax[:, j % 2, :]).then_inc(parts_ready, 1)
                    dve.wait_ge(parts_ready, 2 * s + 1)
                    nc.vector.tensor_tensor(negmax_parts[:, j % 2, :, 1], negmax[:, j % 2, :],
                                            negmax_parts[:, j % 2, :, 0], ALU.subtract).then_inc(parts_ready, 1)
                if j % 2 == 1 and in_range(s, 5, BATCH + 5):
                    t = (s - 5) // 2
                    dve.wait_ge(un_t, t + 1)
                    tile = acc[:, bass.ds(t, 1), :].rearrange("p a f -> p (a f)")
                    nc.vector.tensor_tensor(tile, ps_x[:], tile, ALU.add).then_inc(x_added, 1)
                    dve.wait_ge(x_added, t + 1)
                if in_range(s, 3, BATCH + 3):
                    b3 = (j - 3) % 4
                    dve.wait_ge(pv_done, s - 2)
                    v = ps_v[b3 % 2][:, 0:KC * VC].rearrange("p (n c) -> p n c", n=KC)
                    nc.vector.reciprocal(inv[:, b3 % 2, :], v[:, :, SEQ]).then_inc(inv_ready, 1)
                    dve.wait_ge(inv_ready, s - 2)
                    at = SEQ * (b3 % 2)
                    nc.vector.tensor_tensor(un[:, b3 // 2, :, at:at + SEQ], v[:, :, 0:SEQ],
                                            inv[:, b3 % 2, :].unsqueeze(2).to_broadcast([P, KC, SEQ]),
                                            ALU.mult).then_inc(un_ready, 1)
                if j % 2 == 1 and in_range(s, 5, BATCH + 5):
                    tile_statistics(nc, acc, stats, (s - 5) // 2)

            run(dve, slot, 0, BATCH + 4)

        @block.tensor
        def _(pe):
            pe.wait_ge(fills, FILLS)
            pe.wait_ge(ident_ready, 1)

            def attend(s, j, n):
                if not in_range(s, 3, BATCH + 3):
                    return
                b3 = (j - 3) % 4
                if n == 0:
                    pe.wait_ge(pl_ready, KC * (s - 2))
                    if isinstance(s, int) and s == 3:
                        pe.wait_ge(vtl_ready, KC)
                    if above(s, s - 4):
                        pe.wait_ge(un_ready, s - 4)
                out = ps_v[b3 % 2]
                cols = slice(n * P, (n + 1) * P)
                for mc in range(KC):
                    full, part = out[:, n * VC:(n + 1) * VC], out[:, n * VC:n * VC + SEQ]
                    high = vth[:, mc, bass.ds(s - 3, 1), :].rearrange("p a c -> p (a c)")
                    low = vtl[:, mc, bass.ds(s - 3, 1), :].rearrange("p a c -> p (a c)")
                    p_high, p_low = ph[:, b3 % 2, mc, cols], pl[:, b3 % 2, mc, cols]
                    nc.tensor.matmul(full, p_high, high, start=(mc == 0), stop=False)
                    nc.tensor.matmul(part, p_high, low, start=False, stop=False)
                    m = nc.tensor.matmul(full, p_low, high, start=False, stop=(mc == KC - 1))
                if n == KC - 1:
                    m.then_inc(pv_done, 1)

            def slot(s, j):
                if in_range(s, 1, BATCH + 1):
                    pe.wait_ge(parts_ready, 2 * s)
                    if above(s, s - 1):
                        pe.wait_ge(row_ready, s - 1)
                    for n in range(KC):
                        m = nc.tensor.transpose(ps_n[0:2, n * P:(n + 1) * P],
                                                negmax_parts[:, (j - 1) % 2, n, :], identh[:])
                    m.then_inc(parts_t, 1)
                for mc in range(KC):
                    cols = slice(mc * P, (mc + 1) * P)
                    if in_range(s, 2, BATCH + 2):
                        i = (j - 2) % 4
                        if mc == 0:
                            pe.wait_ge(row_ready, s - 1)
                        c = (s - 2) * KC + mc
                        if above(c, c - 1):
                            pe.wait_ge(exp_ready, c - 1)
                        nc.tensor.matmul(ps_e[mc % 2][:], q_pair[:, i, cols], k_pair[:, i, :], start=True, stop=False)
                        nc.tensor.matmul(ps_e[mc % 2][:], q_high[:, i, cols], k_low[:, i, :], start=False,
                                         stop=True).then_inc(s_done, 1)
                    if in_range(s, 0, BATCH):
                        if mc == 0:
                            pe.wait_ge(low_ready, s + 1)
                        c = s * KC + mc
                        if above(c, c - 1):
                            pe.wait_ge(max_ready, c - 1)
                        nc.tensor.matmul(ps_s[mc % 2][:], k_pair[:, j, cols], q_pair[:, j, :], start=True,
                                         stop=True).then_inc(smax_done, 1)
                    if mc == 1:
                        attend(s, j, 0)
                        attend(s, j, 1)
                        if j % 2 == 1 and in_range(s, 5, BATCH + 5):
                            t = (s - 5) // 2
                            pe.wait_ge(un_ready, s - 3)
                            if above(s, t):
                                pe.wait_ge(x_added, t)
                            for n in range(KC):
                                m = nc.tensor.transpose(ps_x[:, n * P:(n + 1) * P],
                                                        un[:, ((j - 5) % 4) // 2, n, :], ident[:])
                            m.then_inc(un_t, 1)
                attend(s, j, 2)
                attend(s, j, 3)

            run(pe, slot, 0, BATCH + 4)


def feed_forward(nc, keep, ag_d, au_d, ad_d, out_d):
    acc, xth, xtl, ffn_w, ident = keep["acc"], keep["xth"], keep["xtl"], keep["ffn_w"], keep["ident"]
    GT = 4
    GROUPS = TILES // GT
    GTOK = GT * P
    T_AT = {3 + 2 * i: i for i in range(GT)}
    w_gate = ffn_w[:, 0:KC * INTER].rearrange("p (k i) -> p k i", k=KC)
    w_up = ffn_w[:, KC * INTER:2 * KC * INTER].rearrange("p (k i) -> p k i", k=KC)
    w_down = ffn_w[:, 2 * KC * INTER:FFN_W].rearrange("p (c h) -> p c h", c=IC)
    with ExitStack() as ctx:
        def sb(name, shape, dt):
            return ctx.enter_context(nc.sbuf_tensor(name, shape, dt))

        def sem(name):
            return ctx.enter_context(nc.semaphore(name))

        stats = keep["stats"]
        meanvar = sb("meanvar2", [P, TILES, 2], F32)
        work = sb("work2", [P, 4, TILES], F32)
        rstd = sb("rstd2", [P, TILES], F32)
        stats3 = sb("stats3", [P, GT, 6], F32)
        meanvar3 = sb("meanvar3", [P, GT, 2], F32)
        work3 = sb("work3", [P, 4, GT], F32)
        rstd3 = sb("rstd3", [P, GT], F32)
        ag = sb("ag", [P, IC], F32)
        au = sb("au", [P, IC], F32)
        ad = sb("ad", [P, HID], F32)
        gate = sb("gate", [P, 2, GTOK], F32)
        h32 = sb("h32", [P, 2, GTOK], F32)
        hh = sb("hh", [P, 2, GTOK], F16)
        hl = sb("hl", [P, 2, GTOK], F16)
        y = sb("y", [P, GT, HID], F32)
        staged = sb("staged", [P, 2, HID], F32)

        banks = [ctx.enter_context(nc.psum_tensor(f"ps_c{i}", [P, 512], F32)) for i in range(8)]
        ps_g, ps_u, ps_t, ps_d = banks[0:2], banks[2], banks[3], banks[4:8]

        stat, root, stat3, root3 = sem("stat2"), sem("root2"), sem("stat3"), sem("root3")
        small_in = sem("small_in")
        x2_ready, x2_t, x2h_ready, x2l_ready = sem("x2_ready"), sem("x2_t"), sem("x2h_ready"), sem("x2l_ready")
        gu_done, gate_ready, h32_ready, hh_ready, hl_ready = (
            sem("gu_done"), sem("gate_ready"), sem("h32_ready"), sem("hh_ready"), sem("hl_ready"))
        down_done, y_ready, y_added, y_stats = sem("down_done"), sem("y_ready"), sem("y_added"), sem("y_stats")
        x3_ready, out_sent = sem("x3_ready"), sem("out_sent")
        block = ctx.enter_context(nc.Block())

        def rows(ic):
            return P if ic < IC - 1 else ILAST

        def tile_of(t):
            return acc[:, bass.ds(t, 1), :].rearrange("p a f -> p (a f)")

        @block.sync
        def _(sp):
            with nc.allow_non_contiguous_dma("one column per chunk"):
                for v, src in ((ag, ag_d), (au, au_d)):
                    sp.dma_start(v[:, 0:IC - 1], src[0:(IC - 1) * P].rearrange("(c p) -> p c", p=P)
                                 ).then_inc(small_in, 16)
                    sp.dma_start(v[0:ILAST, IC - 1:IC], src[(IC - 1) * P:INTER].rearrange("(p c) -> p c", c=1)
                                 ).then_inc(small_in, 16)
            sp.dma_start(ad[:], ad_d.rearrange("(a f) -> a f", a=1).to_broadcast([P, HID])).then_inc(small_in, 16)
            with sp.Fori(0, TILES, 1) as t:
                sp.wait_ge(x3_ready, t + 1)
                sp.dma_start(out_d[bass.ds(t, 1), :, :].rearrange("a p f -> p (a f)"), tile_of(t)
                             ).then_inc(out_sent, 16)
            sp.wait_ge(out_sent, 16 * TILES)

        @block.scalar
        def _(act):
            act.wait_ge(stat, TILES + 1)
            nc.scalar.activation(work[:, 1, :], work[:, 0, :], ACT.Sqrt).then_inc(root, 1)

            def high(t):
                act.wait_ge(x2_t, t + 1)
                nc.scalar.activation(xth[:, :, bass.ds(t * P, P)], ps_t[:].rearrange("p (k c) -> p k c", k=KC),
                                     ACT.Copy).then_inc(x2h_ready, 1)

            def root_of(g):
                act.wait_ge(stat3, 10 * g + GT + 1)
                nc.scalar.activation(work3[:, 1, :], work3[:, 0, :], ACT.Sqrt).then_inc(root3, 1)

            def group(g, finish, prepare):
                for ic in range(IC):
                    r, par = rows(ic), ic % 2
                    u = g * IC + ic
                    act.wait_ge(gu_done, u + 1)
                    nc.scalar.activation(gate[0:r, par, :], ps_g[par][0:r, :], ACT.Silu,
                                         scale=ag[0:r, ic:ic + 1]).then_inc(gate_ready, 1)
                    act.wait_ge(h32_ready, u + 1)
                    nc.scalar.activation(hh[0:r, par, :], h32[0:r, par, :], ACT.Copy).then_inc(hh_ready, 1)
                    if prepare and ic in T_AT:
                        high((g + 1) * GT + T_AT[ic])
                    if finish and ic == GT + 1:
                        root_of(g - 1)

            for t in range(GT):
                high(t)
            act.wait_ge(small_in, 80)
            group(0, False, True)
            with act.Fori(1, GROUPS - 1, 1) as g:
                group(g, True, True)
            group(GROUPS - 1, True, False)
            root_of(GROUPS - 1)

        @block.vector
        def _(dve):
            n = norm_variance(nc, dve, stats, meanvar, work, stat, 0)
            dve.wait_ge(root, 1)
            norm_rstd(nc, dve, rstd, work, stat, n)

            def norm(t, j):
                if above(t, t - 1):
                    dve.wait_ge(x2_t, t - 1)
                normalise(nc, staged[:, j, :], tile_of(t), meanvar, rstd, t).then_inc(x2_ready, 1)
                normalise(nc, tile_of(t), tile_of(t), meanvar, rstd, t)

            def low(t):
                dve.wait_ge(x2h_ready, t + 1)
                nc.vector.tensor_tensor(xtl[:, :, bass.ds(t * P, P)], ps_t[:].rearrange("p (k c) -> p k c", k=KC),
                                        xth[:, :, bass.ds(t * P, P)], ALU.subtract).then_inc(x2l_ready, 1)

            def scaled(g):
                dve.wait_ge(down_done, g + 1)
                for tt in range(GT):
                    nc.vector.tensor_tensor(y[:, tt, :], ps_d[tt][:], ad[:], ALU.mult).then_inc(y_ready, 1)

            def added(g, tt):
                t = g * GT + tt
                dve.wait_ge(y_ready, t + 1)
                nc.vector.tensor_tensor(tile_of(t), y[:, tt, :], tile_of(t), ALU.add).then_inc(y_added, 1)

            def measured(g, tt):
                nc.vector.bn_stats(stats3[:, tt, :], tile_of(g * GT + tt)).then_inc(y_stats, 1)

            def variance(g):
                norm_variance(nc, dve, stats3, meanvar3, work3, stat3, 10 * g)

            def deviation(g):
                dve.wait_ge(root3, g + 1)
                norm_rstd(nc, dve, rstd3, work3, stat3, 10 * g + GT + 1)

            def send(g, tt):
                t = g * GT + tt
                normalise(nc, tile_of(t), tile_of(t), meanvar3, rstd3, tt).then_inc(x3_ready, 1)

            def group(g, finish, prepare):
                if finish:
                    scaled(g - 1)
                for ic in range(IC):
                    r, par = rows(ic), ic % 2
                    u = g * IC + ic
                    if finish and 1 <= ic <= GT:
                        dve.wait_ge(y_added, (g - 1) * GT + ic)
                    if finish and ic == GT + 1:
                        dve.wait_ge(y_stats, g * GT)
                    dve.wait_ge(gate_ready, u + 1)
                    nc.vector.scalar_tensor_tensor(h32[0:r, par, :], ps_u[0:r, :], au[0:r, ic:ic + 1],
                                                   gate[0:r, par, :], ALU.mult, ALU.mult).then_inc(h32_ready, 1)
                    dve.wait_ge(hh_ready, u + 1)
                    nc.vector.tensor_tensor(hl[0:r, par, :], h32[0:r, par, :], hh[0:r, par, :],
                                            ALU.subtract).then_inc(hl_ready, 1)
                    if prepare:
                        if ic in T_AT:
                            low((g + 1) * GT + T_AT[ic])
                        if ic + 2 in T_AT:
                            norm((g + 1) * GT + T_AT[ic + 2], T_AT[ic + 2] % 2)
                    if finish:
                        if ic < GT:
                            added(g - 1, ic)
                        if 1 <= ic <= GT:
                            measured(g - 1, ic - 1)
                        if ic == GT + 1:
                            variance(g - 1)
                        if ic == GT + 2:
                            deviation(g - 1)
                        if GT + 3 <= ic < 2 * GT + 3:
                            send(g - 1, ic - GT - 3)

            norm(0, 0)
            for t in range(1, GT):
                norm(t, t % 2)
                low(t - 1)
            low(GT - 1)
            dve.wait_ge(small_in, 80)
            group(0, False, True)
            with dve.Fori(1, GROUPS - 1, 1) as g:
                group(g, True, True)
            group(GROUPS - 1, True, False)
            scaled(GROUPS - 1)
            for tt in range(GT):
                added(GROUPS - 1, tt)
                dve.wait_ge(y_added, (GROUPS - 1) * GT + tt + 1)
                measured(GROUPS - 1, tt)
            dve.wait_ge(y_stats, TILES)
            variance(GROUPS - 1)
            deviation(GROUPS - 1)
            for tt in range(GT):
                send(GROUPS - 1, tt)

        @block.tensor
        def _(pe):
            def transpose(t, j):
                pe.wait_ge(x2_ready, t + 1)
                if above(t, t):
                    pe.wait_ge(x2l_ready, t)
                for k in range(KC):
                    m = nc.tensor.transpose(ps_t[:, k * P:(k + 1) * P], staged[:, j, k * P:(k + 1) * P], ident[:])
                m.then_inc(x2_t, 1)

            def down(g, ic):
                r, par = rows(ic), ic % 2
                pe.wait_ge(hl_ready, g * IC + ic + 1)
                for tt in range(GT):
                    if ic == 0 and above(g, GT * (g - 1) + tt + 1):
                        pe.wait_ge(y_ready, GT * (g - 1) + tt + 1)
                    c = slice(tt * P, (tt + 1) * P)
                    nc.tensor.matmul(ps_d[tt][:], hh[0:r, par, c], w_down[0:r, ic, :], start=(ic == 0), stop=False)
                    m = nc.tensor.matmul(ps_d[tt][:], hl[0:r, par, c], w_down[0:r, ic, :], start=False,
                                         stop=(ic == IC - 1))
                if ic == IC - 1:
                    m.then_inc(down_done, 1)

            def project(g, ic, out, w):
                r = rows(ic)
                c = slice(ic * P, ic * P + r)
                for k in range(KC):
                    nc.tensor.matmul(out[0:r, :], w[:, k, c], xth[:, k, bass.ds(g * GTOK, GTOK)],
                                     start=(k == 0), stop=False)
                    m = nc.tensor.matmul(out[0:r, :], w[:, k, c], xtl[:, k, bass.ds(g * GTOK, GTOK)],
                                         start=False, stop=(k == KC - 1))
                return m

            def group(g, prepare):
                pe.wait_ge(x2l_ready, GT * (g + 1))
                for ic in range(IC):
                    u = g * IC + ic
                    if prepare and ic in T_AT:
                        transpose((g + 1) * GT + T_AT[ic], T_AT[ic] % 2)
                    free = u - 1 if ic >= 2 else u - ic
                    if above(g, free):
                        pe.wait_ge(gate_ready, free)
                    project(g, ic, ps_g[ic % 2], w_gate)
                    if above(g, u):
                        pe.wait_ge(h32_ready, u)
                    project(g, ic, ps_u, w_up).then_inc(gu_done, 1)
                    if ic >= 1:
                        down(g, ic - 1)
                down(g, IC - 1)

            for t in range(GT):
                transpose(t, t % 2)
            group(0, True)
            with pe.Fori(1, GROUPS - 1, 1) as g:
                group(g, True)
            group(GROUPS - 1, False)


def decoder_layer(nc, x_nat, x_t, ctx_nat, ctx_t, w_codes, w_scales, ffn_d, ag_d, au_d, ad_d,
                  cos_d, sin_d, mask_d, ident_d, out_d):
    with ExitStack() as ctx:
        def sb(name, shape, dt):
            return ctx.enter_context(nc.sbuf_tensor(name, shape, dt))

        keep = {
            "acc": sb("acc", [P, TILES, HID], F32),
            "xth": sb("xth", [P, KC, TOK], F16),
            "xtl": sb("xtl", [P, KC, TOK], F16),
            "ffn_w": sb("ffn_w", [P, FCH * CHUNK], F16),
            "ident": sb("ident", [P, P], F32),
            "stats": sb("stats", [P, TILES, 6], F32),
        }
        attention(nc, keep, x_nat, x_t, w_codes, w_scales, cos_d, sin_d, mask_d, ident_d, ffn_d)
        cross_attention(nc, keep, ctx_nat, ctx_t)
        feed_forward(nc, keep, ag_d, au_d, ad_d, out_d)


def rotary_tables():
    pos = (np.arange(P) % SEQ).astype(np.float32)
    inv_freq = (1.0 / 10000.0 ** (np.arange(0, HD, 2, dtype=np.float32) / np.float32(HD))).astype(np.float32)
    f = pos[:, None] * inv_freq[None, :]
    c = np.repeat(np.cos(f.astype(np.float64)), 2, axis=1)
    s = np.stack([-np.sin(f.astype(np.float64)), np.sin(f.astype(np.float64))], axis=-1).reshape(P, HD)
    scale = np.array([HD ** -0.5] * REP + [1.0]) / WSCALE
    return ((scale[None, :, None] * c[:, None, :]).reshape(P, ROT).astype(np.float32),
            (scale[None, :, None] * s[:, None, :]).reshape(P, ROT).astype(np.float32))


def causal_mask():
    q, k = (np.arange(P) % SEQ)[:, None], np.arange(SEQ)[None, :]
    return np.where(k <= q, 0.0, -1e30).astype(np.float32)


def pack_group(q, k, v, o):
    parts = [q.reshape(KC, -1, NKV, REP * HD), k.reshape(KC, -1, NKV, HD), v.reshape(KC, -1, NKV, HD)]
    qkv = np.concatenate(parts, axis=3).transpose(2, 1, 0, 3)
    rows = o.reshape(NKV, REP, -1, HID).transpose(0, 2, 1, 3)
    n = qkv.shape[1]
    return np.concatenate([qkv.reshape(NKV, n, -1), rows.reshape(NKV, n, -1)], axis=2)


def by_chunk(a):
    g, n, w = a.shape
    return np.ascontiguousarray(a.reshape(g, n, w // CHUNK, CHUNK).transpose(0, 2, 1, 3).reshape(-1, n, CHUNK))


def pack_ffn(wg, wu, wd):
    down = np.zeros((IC * P, HID), np.float32)
    down[:INTER] = wd.T
    cols = np.concatenate([wg.T.reshape(KC, P, INTER).transpose(1, 0, 2).reshape(P, -1),
                           wu.T.reshape(KC, P, INTER).transpose(1, 0, 2).reshape(P, -1),
                           down.reshape(IC, P, HID).transpose(1, 0, 2).reshape(P, -1),
                           np.zeros((P, FCH * CHUNK - FFN_W), np.float32)], axis=1)
    return by_chunk(cols[None])


def kernel(x, ctx_4096, L0_attn_q_codes, L0_attn_q_scales, L0_attn_k_codes, L0_attn_k_scales,
           L0_attn_v_codes, L0_attn_v_scales, L0_attn_o_codes, L0_attn_o_scales, L0_ffn_Wg, L0_ffn_Wu,
           L0_ffn_Wd, L0_ffn_ag, L0_ffn_au, L0_ffn_ad):
    import concourse.bacc as bacc
    from concourse.bass_utils import run_bass_kernel_spmd

    a = [np.asarray(v) for v in (L0_attn_q_codes, L0_attn_k_codes, L0_attn_v_codes, L0_attn_o_codes)]
    s = [np.asarray(v) for v in (L0_attn_q_scales, L0_attn_k_scales, L0_attn_v_scales, L0_attn_o_scales)]
    x, c = np.asarray(x).reshape(TOK, HID), np.asarray(ctx_4096).reshape(TOK, HID)
    cos, sin = rotary_tables()
    host = {
        "x_nat": x.reshape(TILES, P, HID),
        "x_t": x.T.reshape(KC, P, TOK),
        "ctx_nat": c.reshape(TILES, P, HID),
        "ctx_t": c.T.reshape(KC, P, TOK),
        "w_codes": by_chunk(pack_group(*a)),
        "w_scales": by_chunk(pack_group(*s)).reshape(-1, CHUNK),
        "ffn_d": pack_ffn(np.asarray(L0_ffn_Wg), np.asarray(L0_ffn_Wu), np.asarray(L0_ffn_Wd)),
        "ag_d": np.asarray(L0_ffn_ag), "au_d": np.asarray(L0_ffn_au), "ad_d": np.asarray(L0_ffn_ad),
        "cos_d": cos, "sin_d": sin, "mask_d": causal_mask(), "ident_d": np.eye(P, dtype=np.float32),
    }
    nc = bacc.Bacc("TRN2", target_bir_lowering=False, num_devices=1)
    arrays, args = {}, {}
    for name, v in host.items():
        v = np.ascontiguousarray(v)
        arrays[f"in_{name}"] = v
        args[name] = nc.dram_tensor(f"in_{name}", v.shape, mybir.dt.from_np(v.dtype), kind="ExternalInput").ap()
    args["out_d"] = nc.dram_tensor("out_0", (TILES, P, HID), F32, kind="ExternalOutput").ap()
    decoder_layer(nc, **args)
    r = run_bass_kernel_spmd(nc, [arrays], core_ids=[0])
    return r.results[0]["out_0"].reshape(BATCH, SEQ, HID)
```

```python
import numpy as np
from contextlib import ExitStack

import concourse.bass as bass
from concourse import mybir

F32 = mybir.dt.float32
F16 = mybir.dt.float16
BF16 = mybir.dt.bfloat16
I32 = mybir.dt.int32
ALU = mybir.AluOpType
ACT = mybir.ActivationFunctionType
AX = mybir.AxisListType

P = 128
BATCH, SEQ, HID = 32, 64, 512
NH, NKV, HD = 32, 8, 128
REP = NH // NKV
TOK = BATCH * SEQ
TILES = TOK // P
KC = HID // P
QKV = (REP + 2) * HD
ROT = (REP + 1) * HD
GROUP_W = KC * QKV + REP * HID
CHUNK = 640
NCHUNK = GROUP_W // CHUNK
IN_CHUNKS = -(-KC * QKV // CHUNK)
UNITS = NKV * TILES
STEP = 4
XB = STEP * P
INTER = 1376
IC = -(-INTER // P)
ILAST = INTER - (IC - 1) * P
FFN_W = 2 * KC * INTER + IC * HID
FCH = UNITS // STEP - TILES // STEP
WSCALE = 64.0
EPS = 1e-5


def in_range(n, lo, hi):
    return not isinstance(n, int) or lo <= n < hi


def mine(b):
    return slice(0, SEQ) if b % 2 == 0 else slice(SEQ, P)


def other(b):
    return slice(SEQ, P) if b % 2 == 0 else slice(0, SEQ)


def last(end, step):
    return end - step + 1


def above(n, count):
    return not isinstance(n, int) or count > 0


def attention(nc, keep, x_nat, x_t, w_codes, w_scales, cos_d, sin_d, mask_d, ident_d, ffn_d):
    acc, xth, xtl, ffn_w, ident = keep["acc"], keep["xth"], keep["xtl"], keep["ffn_w"], keep["ident"]
    with ExitStack() as ctx:
        def sb(name, shape, dt):
            return ctx.enter_context(nc.sbuf_tensor(name, shape, dt))

        def pb(name, cols):
            return ctx.enter_context(nc.psum_tensor(name, [P, cols], F32))

        def sem(name):
            return ctx.enter_context(nc.semaphore(name))

        wh = sb("wh", [P, 2 * GROUP_W], F16)
        wl = sb("wl", [P, 2 * GROUP_W], F16)
        codes = sb("codes", [P, 2, CHUNK], I32)
        scales = sb("scales", [P, 2, CHUNK], F32)
        w32 = sb("w32", [P, 2, CHUNK], F32)
        ffn32 = sb("ffn32", [P, CHUNK], F32)
        xt32 = sb("xt32", [P, 2, KC, XB], F32)
        cos = sb("cos", [P, ROT], F32)
        sin = sb("sin", [P, ROT], F32)
        mask32 = sb("mask32", [P, SEQ], F32)
        mask = sb("mask", [P, REP * SEQ], BF16)
        identb = sb("identb", [P, P], BF16)
        rot_c = sb("rot_c", [P, ROT], F32)
        rot_s = sb("rot_s", [P, ROT], F32)
        rot = sb("rot", [P, ROT], F32)
        qkh = sb("qkh", [P, ROT], F16)
        qkl = sb("qkl", [P, ROT], F16)
        vh = sb("vh", [P, 2, HD], F16)
        vl = sb("vl", [P, 2, HD], F16)
        negmax = sb("negmax", [P, 2, REP], F32)
        sums = sb("sums", [P, 2, REP], F32)
        inv = sb("inv", [P, 2, REP], F32)
        prob = sb("prob", [P, REP, SEQ], F32)
        probn = sb("probn", [P, REP, SEQ], F32)
        pth = sb("pth", [P, REP * SEQ], F16)
        ptl = sb("ptl", [P, REP * SEQ], F16)
        oth = sb("oth", [P, 2, REP * P], F16)
        otl = sb("otl", [P, 2, REP * P], F16)

        ps_qkv = pb("ps_qkv", 1024)
        ps_qk = pb("ps_qk", 1024)
        ps_sp = pb("ps_sp", 512)
        ps_s, ps_p = ps_sp[:, 0:REP * SEQ], ps_sp[:, REP * SEQ:2 * REP * SEQ]
        ps_o = pb("ps_o", 1024)
        ps_o_view = ps_o[:].rearrange("p (b r) -> p b r", b=2)[:, :, 0:REP * SEQ].rearrange(
            "p b (h q) -> p b h q", h=REP)
        ps_out = pb("ps_out", 512)

        const_in = sem("const_in")
        xt_in = [sem("xt_in0"), sem("xt_in1")]
        x_in = [sem("x_in_first"), sem("x_in_rest")]
        fills = sem("fills")
        chunk_in = [sem("chunk_in0"), sem("chunk_in1")]
        ffn_in = sem("ffn_in")
        consts = sem("consts")
        xth_ready, xtl_ready = sem("xth_ready"), sem("xtl_ready")
        w32_ready, wh_ready, wl_ready = sem("w32_ready"), sem("wh_ready"), sem("wl_ready")
        ffn_ready = sem("ffn_ready")
        qkv_done, qk_t, scores, p_t, pv_done, out_done = (
            sem("qkv_done"), sem("qk_t"), sem("scores"), sem("p_t"), sem("pv_done"), sem("out_done"))
        rot_parts, rotated = sem("rot_parts"), sem("rotated")
        qkh_ready, qkl_ready = sem("qkh_ready"), sem("qkl_ready")
        vh_ready, vl_ready = sem("vh_ready"), sem("vl_ready")
        max_ready, exp_ready, inv_ready, prob_ready = (
            sem("max_ready"), sem("exp_ready"), sem("inv_ready"), sem("prob_ready"))
        pth_ready, ptl_ready = sem("pth_ready"), sem("ptl_ready")
        oth_ready, otl_ready = sem("oth_ready"), sem("otl_ready")
        acc_added = sem("acc_added")

        def wcol(n, at):
            return (n // TILES) % 2 * GROUP_W + at

        def by_sequence(tile):
            return tile.rearrange("p (h b q) -> p b h q", h=REP, b=2)

        def xcol(n):
            return n % TILES * P

        block = ctx.enter_context(nc.Block())

        @block.sync
        def _(sp):
            def load_chunk(c, buf):
                if above(c, c - 1):
                    sp.wait_ge(w32_ready, c - 1)
                sp.dma_start(codes[:, buf, :], w_codes[bass.ds(c, 1), :, :].rearrange("a p f -> p (a f)")
                             ).then_inc(chunk_in[buf], 16)
                sp.dma_start(scales[:, buf, :], w_scales[bass.ds(c, 1), :].to_broadcast([P, CHUNK])
                             ).then_inc(chunk_in[buf], 16)

            for c in range(NCHUNK + 2):
                load_chunk(c, c % 2)
                if c == NCHUNK // 2:
                    for dst, src in ((cos, cos_d), (sin, sin_d), (mask32, mask_d), (ident, ident_d)):
                        sp.dma_start(dst[:], src).then_inc(const_in, 16)
            first, rest = slice(0, STEP), slice(STEP, TILES)
            sp.dma_start(acc[:, first, :], x_nat[first].rearrange("t p f -> p t f")).then_inc(x_in[0], 16)
            sp.wait_ge(xt_in[0], 32)
            sp.dma_start(acc[:, rest, :], x_nat[rest].rearrange("t p f -> p t f")).then_inc(x_in[1], 16)
            with sp.Fori(NCHUNK + 2, last(NKV * NCHUNK, 2), 2) as c:
                load_chunk(c, 0)
                load_chunk(c + 1, 1)

        @block.gpsimd
        def _(pool):
            def load_x(i):
                if i >= 2:
                    pool.wait_ge(xtl_ready, i - 1)
                pool.dma_start(xt32[:, i % 2], x_t[:, :, i * XB:(i + 1) * XB].rearrange("k p c -> p k c")
                               ).then_inc(xt_in[i % 2], 16)

            load_x(0)

            def slot(n, par, load_ffn):
                if load_ffn is not None:
                    if above(n, load_ffn):
                        pool.wait_ge(ffn_ready, load_ffn)
                    pool.dma_start(ffn32[:], ffn_d[bass.ds(load_ffn, 1), :, :].rearrange("a p f -> p (a f)")
                                   ).then_inc(ffn_in, 16)
                if in_range(n, 1, UNITS + 1):
                    pool.wait_ge(inv_ready, n)
                    if above(n, n - 1):
                        pool.wait_ge(p_t, n - 1)
                    nc.gpsimd.tensor_tensor(
                        probn[:], prob[:],
                        inv[:, 1 - par, :].unsqueeze(2).to_broadcast([P, REP, SEQ]),
                        ALU.mult).then_inc(prob_ready, 1)
                if in_range(n, 0, UNITS):
                    pool.wait_ge(rot_parts, 2 * n + 2)
                    if above(n, n):
                        pool.wait_ge(qk_t, n)
                    nc.gpsimd.tensor_tensor(rot[:], rot_c[:], rot_s[:], ALU.add).then_inc(rotated, 1)

            def body(n0, ffn):
                for j in range(STEP):
                    slot(n0 + j, j % 2, n0 // STEP if ffn and j == 0 else None)

            q_high, k_low = keep["q_high"], keep["k_low"]
            filled = 0
            for what, value in [(q_high[:], 0.0), (k_low[:], 0.0)] + [
                    (q_high[other(i).start:other(i).start + 2, i, :], 1.0) for i in range(4)]:
                if filled:
                    pool.wait_ge(fills, filled)
                nc.gpsimd.memset(what, value).then_inc(fills, 1)
                filled += 1
            slot(0, 0, 0)
            pool.wait_ge(w32_ready, NCHUNK)
            load_x(1)
            load_x(2)
            for j in range(1, STEP):
                slot(j, j % 2, None)
                if 2 < j + 1 < TOK // XB:
                    load_x(j + 1)
            with pool.Fori(STEP, last(UNITS - TILES, STEP), STEP) as n0:
                body(n0, True)
            with pool.Fori(UNITS - TILES, last(UNITS, STEP), STEP) as n0:
                body(n0, False)
            slot(UNITS, 0, None)

        @block.scalar
        def _(act):
            def chunk_high(c, buf):
                act.wait_ge(w32_ready, c + 1)
                nc.scalar.activation(wh[:, bass.ds(c % (2 * NCHUNK) * CHUNK, CHUNK)], w32[:, buf, :],
                                     ACT.Copy, scale=WSCALE).then_inc(wh_ready, 1)

            def x_high(i):
                act.wait_ge(xt_in[i % 2], 16 * (i // 2 + 1))
                nc.scalar.activation(xth[:, :, i * XB:(i + 1) * XB], xt32[:, i % 2], ACT.Copy).then_inc(xth_ready, 1)

            for c in range(IN_CHUNKS):
                chunk_high(c, c % 2)
                if c == 0:
                    x_high(0)
            act.wait_ge(const_in, 64)
            nc.scalar.activation(identb[:], ident[:], ACT.Copy)
            nc.scalar.activation(mask[:].rearrange("p (h k) -> p h k", h=REP),
                                 mask32[:].unsqueeze(1).to_broadcast([P, REP, SEQ]), ACT.Copy).then_inc(consts, 1)

            def slot(n, par, chunk, buf):
                if in_range(n, 1, UNITS + 1):
                    act.wait_ge(qk_t, n)
                    nc.scalar.activation(qkh[:], ps_qk[:, 0:ROT], ACT.Copy).then_inc(qkh_ready, 1)
                    act.wait_ge(max_ready, n)
                    if above(n, n - 1):
                        act.wait_ge(prob_ready, n - 1)
                    for h in range(REP):
                        e = nc.scalar.activation(prob[:, h, :], ps_s[:, h * SEQ:(h + 1) * SEQ], ACT.Exp,
                                                 bias=negmax[:, 1 - par, h:h + 1],
                                                 accum_out=sums[:, 1 - par, h:h + 1])
                    e.then_inc(exp_ready, 1)
                if chunk is not None:
                    chunk_high(chunk, buf)
                if in_range(n, 1, UNITS + 1):
                    act.wait_ge(p_t, n)
                    if above(n, n - 1):
                        act.wait_ge(pv_done, n - 1)
                    nc.scalar.activation(pth[:], ps_p, ACT.Copy).then_inc(pth_ready, 1)
                if in_range(n, 0, UNITS):
                    act.wait_ge(rot_parts, 2 * n + 2)
                    if above(n, n - 1):
                        act.wait_ge(pv_done, n - 1)
                    nc.scalar.activation(vh[:, par, :], ps_qkv[:, ROT:QKV], ACT.Copy,
                                         scale=1.0 / WSCALE).then_inc(vh_ready, 1)
                if in_range(n, 1, UNITS + 1):
                    act.wait_ge(pv_done, n)
                    nc.scalar.activation(by_sequence(oth[:, 1 - par, :]), ps_o_view, ACT.Copy).then_inc(oth_ready, 1)

            def body(n0, chunks, first=0):
                for j in range(first, STEP):
                    slot(n0 + j, j % 2, n0 // 2 + NCHUNK + j // 2 if chunks and j % 2 == 0 else None, j // 2)
                    if first:
                        x_high(j)
                    if chunks and j == 3:
                        act.wait_ge(ffn_in, n0 // STEP * 16 + 16)
                        nc.scalar.activation(ffn_w[:, bass.ds(n0 // STEP * CHUNK, CHUNK)], ffn32[:],
                                             ACT.Copy).then_inc(ffn_ready, 1)

            slot(0, 0, None, 0)
            for c in range(IN_CHUNKS, NCHUNK + 1):
                chunk_high(c, c % 2)
            body(0, True, 1)
            with act.Fori(STEP, last(UNITS - TILES, STEP), STEP) as n0:
                body(n0, True)
            with act.Fori(UNITS - TILES, last(UNITS, STEP), STEP) as n0:
                body(n0, False)
            slot(UNITS, 0, None, 0)

        @block.vector
        def _(dve):
            def dequantise(c, buf):
                dve.wait_ge(chunk_in[buf], c // 2 * 32 + 32)
                if above(c, c - 1):
                    dve.wait_ge(wh_ready, c - 1)
                    dve.wait_ge(wl_ready, c - 1)
                nc.vector.scalar_tensor_tensor(w32[:, buf, :], codes[:, buf, :], -8.0, scales[:, buf, :],
                                               ALU.add, ALU.mult).then_inc(w32_ready, 1)

            def chunk_low(c, buf):
                dve.wait_ge(wh_ready, c + 1)
                at = bass.ds(c % (2 * NCHUNK) * CHUNK, CHUNK)
                nc.vector.scalar_tensor_tensor(wl[:, at], w32[:, buf, :], WSCALE, wh[:, at],
                                               ALU.mult, ALU.subtract).then_inc(wl_ready, 1)

            def x_low(i):
                dve.wait_ge(xth_ready, i + 1)
                at = slice(i * XB, (i + 1) * XB)
                nc.vector.tensor_tensor(xtl[:, :, at], xt32[:, i % 2], xth[:, :, at],
                                        ALU.subtract).then_inc(xtl_ready, 1)

            dequantise(0, 0)
            for c in range(IN_CHUNKS):
                if c + 1 < IN_CHUNKS:
                    dequantise(c + 1, (c + 1) % 2)
                chunk_low(c, c % 2)
                if c == 0:
                    x_low(0)

            def slot(n, par, chunk, buf, final=False):
                if in_range(n, 1, UNITS + 1):
                    dve.wait_ge(qkh_ready, n)
                    nc.vector.tensor_tensor(qkl[:], ps_qk[:, 0:ROT], qkh[:], ALU.subtract).then_inc(qkl_ready, 1)
                if in_range(n, 3, UNITS + 3):
                    dve.wait_ge(out_done, n - 2)
                    if isinstance(n, int) and n == 3:
                        dve.wait_ge(x_in[0], 16)
                    if above(n, n - 3):
                        dve.wait_ge(acc_added, n - 3)
                    tile = acc[:, bass.ds((n + 2 * TILES - 3) % TILES, 1), :].rearrange("p a f -> p (a f)")
                    nc.vector.scalar_tensor_tensor(tile, ps_out[:], 1.0 / WSCALE, tile,
                                                   ALU.mult, ALU.add).then_inc(acc_added, 1)
                if in_range(n, 1, UNITS + 1):
                    dve.wait_ge(scores, n)
                    nc.vector.tensor_reduce(negmax[:, 1 - par, :], ps_s.rearrange("p (h k) -> p h k", h=REP),
                                            AX.X, ALU.max, negate=True).then_inc(max_ready, 1)
                if chunk is not None:
                    if above(n, n):
                        dve.wait_ge(qkv_done, n)
                    if above(n, n - 2):
                        dve.wait_ge(out_done, n - 2)
                    dequantise(chunk, buf)
                if final:
                    dve.wait_ge(acc_added, n - 2)
                if in_range(n, 1, UNITS + 1):
                    dve.wait_ge(exp_ready, n)
                    nc.vector.reciprocal(inv[:, 1 - par, :], sums[:, 1 - par, :]).then_inc(inv_ready, 1)
                if final:
                    tile_statistics(nc, acc, keep["stats"], (n + 2 * TILES - 3) % TILES)
                if in_range(n, 0, UNITS):
                    if isinstance(n, int) and n == 0:
                        dve.wait_ge(const_in, 64)
                    dve.wait_ge(qkv_done, n + 1)
                    if above(n, n):
                        dve.wait_ge(rotated, n)
                    nc.vector.tensor_tensor(rot_c[:], ps_qkv[:, 0:ROT], cos[:], ALU.mult).then_inc(rot_parts, 1)
                    src = ps_qkv[:, 0:ROT].rearrange("p (i two) -> p two i", two=2)
                    dst = rot_s[:].rearrange("p (i two) -> p two i", two=2)
                    tab = sin[:].rearrange("p (i two) -> p two i", two=2)
                    nc.vector.tensor_tensor(dst, src[:, ::-1, :], tab, ALU.mult).then_inc(rot_parts, 1)
                if in_range(n, 1, UNITS + 1):
                    dve.wait_ge(pth_ready, n)
                    nc.vector.tensor_tensor(ptl[:], ps_p, pth[:], ALU.subtract).then_inc(ptl_ready, 1)
                if in_range(n, 0, UNITS):
                    dve.wait_ge(vh_ready, n + 1)
                    if above(n, n - 1):
                        dve.wait_ge(pv_done, n - 1)
                    nc.vector.scalar_tensor_tensor(vl[:, par, :], ps_qkv[:, ROT:QKV], 1.0 / WSCALE,
                                                   vh[:, par, :], ALU.mult, ALU.subtract).then_inc(vl_ready, 1)
                if chunk is not None:
                    chunk_low(chunk, buf)
                if in_range(n, 1, UNITS + 1):
                    dve.wait_ge(oth_ready, n)
                    nc.vector.tensor_tensor(by_sequence(otl[:, 1 - par, :]), ps_o_view,
                                            by_sequence(oth[:, 1 - par, :]), ALU.subtract).then_inc(otl_ready, 1)

            def body(n0, chunks):
                for j in range(STEP):
                    slot(n0 + j, j % 2, n0 // 2 + NCHUNK + j // 2 if chunks and j % 2 == 0 else None, j // 2,
                         not chunks)

            slot(0, 0, None, 0)
            dequantise(IN_CHUNKS, IN_CHUNKS % 2)
            for c in range(IN_CHUNKS, NCHUNK + 1):
                if c < NCHUNK:
                    dequantise(c + 1, (c + 1) % 2)
                chunk_low(c, c % 2)
            for j in range(1, STEP):
                slot(j, j % 2, NCHUNK + j // 2 if j % 2 == 0 else None, j // 2)
                x_low(j)
            dve.wait_ge(x_in[1], 16)
            with dve.Fori(STEP, last(UNITS - TILES, STEP), STEP) as n0:
                body(n0, True)
            with dve.Fori(UNITS - TILES, last(UNITS, STEP), STEP) as n0:
                body(n0, False)
            for n in range(UNITS, UNITS + 3):
                slot(n, n % 2, None, 0, True)

        @block.tensor
        def _(pe):
            def slot(n, par):
                first = isinstance(n, int) and n == 0

                def qkv(chunks):
                    for k in chunks:
                        if first:
                            pe.wait_ge(wl_ready, -(-(k + 1) * QKV // CHUNK))
                        for w_at, width, ps_at in ((0, 512, 0), (512, QKV - 512, 512)):
                            at = bass.ds(wcol(n, k * QKV + w_at), width)
                            out = ps_qkv[:, ps_at:ps_at + width]
                            xh = xth[:, k, bass.ds(xcol(n), P)]
                            xl = xtl[:, k, bass.ds(xcol(n), P)]
                            nc.tensor.matmul(out, xh, wh[:, at], start=(k == 0), stop=False)
                            nc.tensor.matmul(out, xh, wl[:, at], start=False, stop=False)
                            m = nc.tensor.matmul(out, xl, wh[:, at], start=False, stop=(k == KC - 1))
                    return m

                if in_range(n, 0, UNITS):
                    if first:
                        pe.wait_ge(xtl_ready, 1)
                    elif isinstance(n, int) and n == 1:
                        pe.wait_ge(wl_ready, IN_CHUNKS)
                    else:
                        pe.wait_ge(wl_ready, n // TILES * NCHUNK + NCHUNK)
                    if above(n, n):
                        pe.wait_ge(vl_ready, n)
                    qkv(range(KC // 2))
                if in_range(n, 1, UNITS + 1):
                    if above(n, n - 1):
                        pe.wait_ge(ptl_ready, n - 1)
                    nc.tensor.matmul(ps_s, identb[:], mask[:], start=True, stop=False)
                    parts = [(ps_s[:, i * SEQ:(i + 1) * SEQ], slice(i * P, (i + 1) * P),
                              slice(REP * P + i % 2 * SEQ, REP * P + (i % 2 + 1) * SEQ)) for i in range(REP)]
                    pe.wait_ge(qkh_ready, n)
                    for out, q, k in parts:
                        nc.tensor.matmul(out, qkh[:, q], qkh[:, k], start=False, stop=False)
                    pe.wait_ge(qkl_ready, n)
                    for i, (out, q, k) in enumerate(parts):
                        nc.tensor.matmul(out, qkh[:, q], qkl[:, k], start=False, stop=False)
                        m = nc.tensor.matmul(out, qkl[:, q], qkh[:, k], start=False, stop=(i == REP - 1))
                    m.then_inc(scores, 1)
                if in_range(n, 0, UNITS):
                    qkv(range(KC // 2, KC)).then_inc(qkv_done, 1)

                def project(h):
                    if not in_range(n, 2, UNITS + 2):
                        return
                    if h == 0:
                        pe.wait_ge(otl_ready, n - 1)
                        if above(n, n - 2):
                            pe.wait_ge(acc_added, n - 2)
                    w = bass.ds(wcol(n + 2 * TILES - 2, KC * QKV + h * HID), HID)
                    oh = oth[:, par, h * P:(h + 1) * P]
                    nc.tensor.matmul(ps_out[:], oh, wh[:, w], start=(h == 0), stop=False)
                    nc.tensor.matmul(ps_out[:], oh, wl[:, w], start=False, stop=False)
                    m = nc.tensor.matmul(ps_out[:], otl[:, par, h * P:(h + 1) * P], wh[:, w],
                                         start=False, stop=(h == REP - 1))
                    if h == REP - 1:
                        m.then_inc(out_done, 1)

                project(0)
                project(1)
                if in_range(n, 1, UNITS + 1):
                    pe.wait_ge(prob_ready, n)
                    if above(n, n - 1):
                        pe.wait_ge(ptl_ready, n - 1)
                    for pair in range(REP // 2):
                        m = nc.tensor.transpose(ps_p[:, pair * P:(pair + 1) * P], probn[:, 2 * pair:2 * pair + 2, :]
                                                .rearrange("p b k -> p (b k)"), ident[:])
                    m.then_inc(p_t, 1)

                project(2)
                project(3)
                if in_range(n, 1, UNITS + 1):
                    pe.wait_ge(pth_ready, n)
                    pe.wait_ge(vl_ready, n)
                    if above(n, n - 1):
                        pe.wait_ge(otl_ready, n - 1)
                    seqs = [(slice(b * SEQ, (b + 1) * SEQ), ps_o[:, 512 * b:512 * b + REP * SEQ]) for b in range(2)]
                    for v in (vh, vl):
                        for own, out in seqs:
                            nc.tensor.matmul(out, v[own, 1 - par, :], pth[own, :], start=(v is vh), stop=False)
                    pe.wait_ge(ptl_ready, n)
                    for own, out in seqs:
                        m = nc.tensor.matmul(out, vh[own, 1 - par, :], ptl[own, :], start=False, stop=True)
                    m.then_inc(pv_done, 1)
                if in_range(n, 0, UNITS):
                    pe.wait_ge(rotated, n + 1)
                    if above(n, n):
                        pe.wait_ge(qkl_ready, n)
                    if first:
                        pe.wait_ge(consts, 1)
                    for h in range(REP):
                        pair = ps_qk[:, h // 2 * 2 * P:(h // 2 + 1) * 2 * P]
                        nc.tensor.transpose(pair.rearrange("p (b h q) -> p h b q", b=2, h=2)[:, h % 2],
                                            rot[:, h * P:(h + 1) * P], ident[:])
                    nc.tensor.transpose(ps_qk[:, REP * P:ROT], rot[:, REP * P:ROT], ident[:]).then_inc(qk_t, 1)

            for n in range(STEP):
                slot(n, n % 2)
            pe.wait_ge(xtl_ready, 2)
            with pe.Fori(STEP, last(UNITS, STEP), STEP) as n0:
                for j in range(STEP):
                    slot(n0 + j, j % 2)
            for n in range(UNITS, UNITS + 2):
                slot(n, n % 2)


def tile_statistics(nc, acc, stats, t):
    return nc.vector.bn_stats(stats[:, bass.ds(t, 1), :].rearrange("p a f -> p (a f)"),
                              acc[:, bass.ds(t, 1), :].rearrange("p a f -> p (a f)"))


def norm_variance(nc, dve, stats, meanvar, work, sem_dve, count):
    n = work.shape[2]
    for t in range(n):
        nc.vector.bn_aggr(meanvar[:, t, :], stats[:, t, :]).then_inc(sem_dve, 1)
    dve.wait_ge(sem_dve, count + n)
    nc.vector.tensor_scalar(work[:, 0, :], meanvar[:, :, 1], EPS, None, ALU.add).then_inc(sem_dve, 1)
    return count + n + 1


def norm_rstd(nc, dve, rstd, work, sem_dve, count):
    def step(ins, n):
        ins.then_inc(sem_dve, 1)
        dve.wait_ge(sem_dve, n)

    v, root, r, a = (work[:, i, :] for i in range(4))
    step(nc.vector.reciprocal(r, root), count + 1)
    step(nc.vector.tensor_tensor(a, r, r, ALU.mult), count + 2)
    step(nc.vector.tensor_tensor(root, a, v, ALU.mult), count + 3)
    step(nc.vector.tensor_scalar(a, root, -0.5, 1.5, ALU.mult, ALU.add), count + 4)
    step(nc.vector.tensor_tensor(rstd[:], r, a, ALU.mult), count + 5)
    return count + 5


def normalise(nc, out, tile, meanvar, rstd, t):
    mean = meanvar[:, bass.ds(t, 1), 0:1].rearrange("p a f -> p (a f)")
    return nc.vector.tensor_scalar(out, tile, mean, rstd[:, bass.ds(t, 1)], ALU.subtract, ALU.mult)


def cross_attention(nc, keep, ctx_nat, ctx_t):
    acc, ident = keep["acc"], keep["ident"]
    SCALE = float(SEQ) ** -0.5
    VC = SEQ + 1
    with ExitStack() as ctx:
        def sb(name, shape, dt):
            return ctx.enter_context(nc.sbuf_tensor(name, shape, dt))

        def pb(name, cols, dt=F32):
            return ctx.enter_context(nc.psum_tensor(name, [P, cols], dt))

        def sem(name):
            return ctx.enter_context(nc.semaphore(name))

        stats = keep["stats"]
        meanvar = sb("meanvar1", [P, TILES, 2], F32)
        work = sb("work1", [P, 4, TILES], F32)
        rstd = sb("rstd1", [P, TILES], F32)
        identh = sb("identh", [P, P], F16)
        ct32 = sb("ct32", [P, KC, TOK], F32)
        vth = sb("vth", [P, KC, BATCH, VC], F16)
        vtl = keep["xtl"][:].rearrange("p k (b c) -> p k b c", b=BATCH)
        ctx32 = sb("ctx32", [P, 2, HID], F32)
        q_pair = sb("q_pair", [P, 4, HID], F16)
        k_pair = sb("k_pair", [P, 4, HID], F16)
        q_high, k_low = keep["q_high"], keep["k_low"]
        negmax = sb("negmax1", [P, 2, KC], F32)
        negmax_parts = sb("negmax_parts", [P, 2, KC, 2], F16)
        e32 = sb("e32", [P, KC, HID], F32)
        ph = sb("ph", [P, 2, KC, HID], F16)
        pl = sb("pl", [P, 2, KC, HID], F16)
        inv = sb("inv1", [P, 2, KC], F32)
        un = sb("un", [P, 2, KC, P], F32)

        ps_s = [pb("ps_smax0", HID), pb("ps_smax1", HID)]
        ps_e = [pb("ps_e0", HID), pb("ps_e1", HID)]
        ps_v = [pb("ps_v0", HID), pb("ps_v1", HID)]
        ps_n = pb("ps_n", 1024, F16)
        ps_x = pb("ps_x", HID)

        stat = sem("stat1")
        root = sem("root1")
        ct_in = [sem(f"ct_in{k}") for k in range(KC)]
        vth_ready, vtl_ready = sem("vth_ready"), [sem(f"vtl_ready{k}") for k in range(KC)]
        ctx_in = [sem("ctx_in0"), sem("ctx_in1")]
        ones_ready = sem("ones_ready")
        ident_ready = sem("ident_ready")
        x1_ready = sem("x1_ready")
        high_ready, low_ready, k_low_ready = sem("high_ready"), sem("low_ready"), sem("k_low_ready")
        smax_done, max_ready, parts_ready, parts_t, row_ready = (
            sem("smax_done"), sem("max_ready1"), sem("parts_ready"), sem("parts_t"), sem("row_ready"))
        s_done, exp_ready, ph_ready, pl_ready = sem("s_done"), sem("exp_ready1"), sem("ph_ready"), sem("pl_ready")
        pv_done, inv_ready, un_ready, un_t, x_added = (
            sem("pv_done1"), sem("inv_ready1"), sem("un_ready"), sem("un_t"), sem("x_added"))

        block = ctx.enter_context(nc.Block())

        def run(eng, slot, first, end, peel=4):
            for s in range(first, peel):
                slot(s, s % 4)
            with eng.Fori(peel, last(BATCH - 4, 4), 4) as s0:
                for j in range(4):
                    slot(s0 + j, j)
            for s in range(BATCH - 4, end):
                slot(s, s % 4)

        @block.sync
        def _(sp):
            def load(t, buf):
                if above(t, 2 * t - 2):
                    sp.wait_ge(k_low_ready, 2 * t - 2)
                sp.dma_start(ctx32[:, buf, :], ctx_nat[bass.ds(t, 1), :, :].rearrange("a p f -> p (a f)")
                             ).then_inc(ctx_in[buf], 16)

            load(0, 0)
            load(1, 1)
            for k in range(KC):
                sp.dma_start(ct32[:, k, :], ctx_t[k, :, :]).then_inc(ct_in[k], 16)
            with sp.Fori(2, last(TILES, 2), 2) as t:
                load(t, 0)
                load(t + 1, 1)

        @block.gpsimd
        def _(pool):
            nc.gpsimd.memset(vth[:, :, :, SEQ:VC], 1.0).then_inc(ones_ready, 1)

            def prepare(b, j):
                pool.wait_ge(high_ready, 2 * b + 2)
                nc.gpsimd.tensor_tensor(k_low[mine(j), j, :], ctx32[mine(j), j // 2, :],
                                        k_pair[mine(j), j, :], ALU.subtract).then_inc(k_low_ready, 1)
                pool.wait_ge(k_low_ready, b + 1)

            pool.wait_ge(ones_ready, 1)
            prepare(0, 0)

            def ctx_low(k):
                pool.wait_ge(vth_ready, k + 1)
                nc.gpsimd.tensor_tensor(vtl[:, k, :, :], ct32[:, k, :].rearrange("p (b c) -> p b c", b=BATCH),
                                        vth[:, k, :, 0:SEQ], ALU.subtract).then_inc(vtl_ready[k], 1)

            def slot(s, j):
                if in_range(s, 2, BATCH + 2):
                    for mc in range(KC):
                        pool.wait_ge(ph_ready, (s - 2) * KC + mc + 1)
                        nc.gpsimd.tensor_tensor(pl[:, j % 2, mc, :], e32[:, mc, :], ph[:, j % 2, mc, :],
                                                ALU.subtract).then_inc(pl_ready, 1)
                        if mc == 1 and in_range(s, 0, BATCH - 1):
                            pool.wait_ge(pl_ready, (s - 2) * KC + 2)
                            prepare(s + 1, (j + 1) % 4)
                elif in_range(s, 0, BATCH - 1):
                    prepare(s + 1, (j + 1) % 4)
                if isinstance(s, int) and s < 2:
                    ctx_low(s + 1)
                    pool.wait_ge(vtl_ready[s + 1], 1)

            run(pool, slot, 0, BATCH + 2)

        @block.scalar
        def _(act):
            nc.scalar.activation(identh[:], ident[:], ACT.Copy).then_inc(ident_ready, 1)
            act.wait_ge(stat, TILES + 1)
            nc.scalar.activation(work[:, 1, :], work[:, 0, :], ACT.Sqrt).then_inc(root, 1)

            def prepare(b, j, part):
                if part == 0:
                    act.wait_ge(x1_ready, b // 2 + 1)
                    if above(b, KC * (b - 3)):
                        act.wait_ge(s_done, KC * (b - 3))
                    nc.scalar.activation(q_pair[mine(j), j, :], acc[mine(j), bass.ds(b // 2, 1), :]
                                         .rearrange("p a f -> p (a f)"), ACT.Copy).then_inc(high_ready, 1)
                else:
                    act.wait_ge(ctx_in[j // 2], b // 4 * 16 + 16)
                    nc.scalar.activation(k_pair[mine(j), j, :], ctx32[mine(j), j // 2, :],
                                         ACT.Copy).then_inc(high_ready, 1)

            def ctx_high(k):
                act.wait_ge(ct_in[k], 16)
                nc.scalar.activation(vth[:, k, :, 0:SEQ], ct32[:, k, :].rearrange("p (b c) -> p b c", b=BATCH),
                                     ACT.Copy).then_inc(vth_ready, 1)

            prepare(0, 0, 0)
            prepare(0, 0, 1)

            def slot(s, j):
                for mc in range(KC + 1):
                    if mc < KC and in_range(s, 2, BATCH + 2):
                        c = (s - 2) * KC + mc
                        act.wait_ge(s_done, c + 1)
                        if above(c, c - KC + 1):
                            act.wait_ge(pl_ready, c - KC + 1)
                        nc.scalar.activation(e32[:, mc, :], ps_e[mc % 2][:], ACT.Exp,
                                             scale=SCALE).then_inc(exp_ready, 1)
                    if mc > 0 and in_range(s, 2, BATCH + 2):
                        if mc == 1 and above(s, s - 3):
                            act.wait_ge(pv_done, s - 3)
                        act.wait_ge(exp_ready, (s - 2) * KC + mc)
                        nc.scalar.activation(ph[:, j % 2, mc - 1, :], e32[:, mc - 1, :], ACT.Copy).then_inc(ph_ready, 1)
                    if mc in (1, 2) and in_range(s, 0, BATCH - 1):
                        prepare(s + 1, (j + 1) % 4, mc - 1)
                if isinstance(s, int) and s < 2:
                    ctx_high(2 * s)
                    ctx_high(2 * s + 1)

            run(act, slot, 0, BATCH + 2)

        @block.vector
        def _(dve):
            done = norm_variance(nc, dve, stats, meanvar, work, stat, 0)
            dve.wait_ge(root, 1)
            norm_rstd(nc, dve, rstd, work, stat, done)

            def norm(t):
                tile = acc[:, bass.ds(t, 1), :].rearrange("p a f -> p (a f)")
                normalise(nc, tile, tile, meanvar, rstd, t).then_inc(x1_ready, 1)

            norm(0)
            norm(1)
            def prepare(b, j, part):
                if part == 0:
                    dve.wait_ge(high_ready, 2 * b + 1)
                    dve.wait_ge(x1_ready, b // 2 + 1)
                    nc.vector.tensor_tensor(q_pair[other(j), j, :], acc[mine(j), bass.ds(b // 2, 1), :]
                                            .rearrange("p a f -> p (a f)"), q_pair[mine(j), j, :], ALU.subtract)
                elif part == 1:
                    nc.vector.tensor_copy(q_high[mine(j), j, :], q_pair[mine(j), j, :])
                else:
                    dve.wait_ge(high_ready, 2 * b + 2)
                    nc.vector.tensor_copy(k_pair[other(j), j, :], k_pair[mine(j), j, :]).then_inc(low_ready, 1)

            for part in range(3):
                prepare(0, 0, part)

            def slot(s, j):
                if j % 2 == 1 and in_range(s, 0, BATCH - 4):
                    norm((s + 3) // 2)
                for mc in range(KC):
                    if in_range(s, 0, BATCH):
                        dve.wait_ge(smax_done, s * KC + mc + 1)
                        nc.vector.tensor_reduce(negmax[:, j % 2, mc:mc + 1], ps_s[mc % 2][:], AX.X, ALU.max,
                                                negate=True).then_inc(max_ready, 1)
                    if mc > 0 and in_range(s, 0, BATCH - 1):
                        prepare(s + 1, (j + 1) % 4, mc - 1)
                    if mc == 0 and j % 2 == 0 and in_range(s, 6, BATCH + 6):
                        t = (s - 6) // 2
                        dve.wait_ge(un_t, t + 1)
                        tile = acc[:, bass.ds(t, 1), :].rearrange("p a f -> p (a f)")
                        nc.vector.tensor_tensor(tile, ps_x[:], tile, ALU.add).then_inc(x_added, 1)
                        dve.wait_ge(x_added, t + 1)
                    if mc == 0 and in_range(s, 4, BATCH + 4):
                        dve.wait_ge(pv_done, s - 3)
                        v = ps_v[j % 2][:, 0:KC * VC].rearrange("p (n c) -> p n c", n=KC)
                        nc.vector.reciprocal(inv[:, j % 2, :], v[:, :, SEQ]).then_inc(inv_ready, 1)
                        dve.wait_ge(inv_ready, s - 3)
                        at = SEQ * (j % 2)
                        nc.vector.tensor_tensor(un[:, j // 2, :, at:at + SEQ], v[:, :, 0:SEQ],
                                                inv[:, j % 2, :].unsqueeze(2).to_broadcast([P, KC, SEQ]),
                                                ALU.mult).then_inc(un_ready, 1)
                    if mc == 0 and j % 2 == 0 and in_range(s, 6, BATCH + 6):
                        tile_statistics(nc, acc, stats, (s - 6) // 2)
                    if mc == 2 and in_range(s, 1, BATCH + 1):
                        dve.wait_ge(parts_t, s)
                        b1 = (j - 1) % 4
                        at = other(b1).start
                        nc.vector.tensor_copy(k_low[at:at + 2, b1, :], ps_n[0:2, 0:HID]).then_inc(row_ready, 1)
                if in_range(s, 0, BATCH):
                    dve.wait_ge(max_ready, KC * (s + 1))
                    if above(s, s - 1):
                        dve.wait_ge(parts_t, s - 1)
                    nc.vector.tensor_copy(negmax_parts[:, j % 2, :, 0], negmax[:, j % 2, :]).then_inc(parts_ready, 1)
                    dve.wait_ge(parts_ready, 2 * s + 1)
                    nc.vector.tensor_tensor(negmax_parts[:, j % 2, :, 1], negmax[:, j % 2, :],
                                            negmax_parts[:, j % 2, :, 0], ALU.subtract).then_inc(parts_ready, 1)
                if isinstance(s, int) and s < 2:
                    k = 3 * s
                    dve.wait_ge(vth_ready, k + 1)
                    nc.vector.tensor_tensor(vtl[:, k, :, :], ct32[:, k, :].rearrange("p (b c) -> p b c", b=BATCH),
                                            vth[:, k, :, 0:SEQ], ALU.subtract).then_inc(vtl_ready[k], 1)

            run(dve, slot, 0, BATCH + 5, peel=8)

        @block.tensor
        def _(pe):
            pe.wait_ge(ones_ready, 1)
            pe.wait_ge(ident_ready, 1)

            def attend(s, j, n):
                if not in_range(s, 3, BATCH + 3):
                    return
                b3 = (j - 3) % 4
                if n == 0:
                    pe.wait_ge(pl_ready, KC * (s - 2))
                    if isinstance(s, int) and s == 3:
                        for k in range(KC):
                            pe.wait_ge(vtl_ready[k], 1)
                    if above(s, s - 4):
                        pe.wait_ge(un_ready, s - 4)
                out = ps_v[b3 % 2]
                cols = slice(n * P, (n + 1) * P)
                for mc in range(KC):
                    full, part = out[:, n * VC:(n + 1) * VC], out[:, n * VC:n * VC + SEQ]
                    high = vth[:, mc, bass.ds(s - 3, 1), :].rearrange("p a c -> p (a c)")
                    low = vtl[:, mc, bass.ds(s - 3, 1), :].rearrange("p a c -> p (a c)")
                    p_high, p_low = ph[:, b3 % 2, mc, cols], pl[:, b3 % 2, mc, cols]
                    nc.tensor.matmul(full, p_high, high, start=(mc == 0), stop=False)
                    nc.tensor.matmul(part, p_high, low, start=False, stop=False)
                    m = nc.tensor.matmul(full, p_low, high, start=False, stop=(mc == KC - 1))
                if n == KC - 1:
                    m.then_inc(pv_done, 1)

            def slot(s, j):
                for mc in range(KC):
                    cols = slice(mc * P, (mc + 1) * P)
                    if in_range(s, 2, BATCH + 2):
                        i = (j - 2) % 4
                        if mc == 0:
                            pe.wait_ge(row_ready, s - 1)
                            pe.wait_ge(k_low_ready, s - 1)
                        c = (s - 2) * KC + mc
                        if above(c, c - 1):
                            pe.wait_ge(exp_ready, c - 1)
                        nc.tensor.matmul(ps_e[mc % 2][:], q_pair[:, i, cols], k_pair[:, i, :], start=True, stop=False)
                        nc.tensor.matmul(ps_e[mc % 2][:], q_high[:, i, cols], k_low[:, i, :], start=False,
                                         stop=True).then_inc(s_done, 1)
                    if in_range(s, 0, BATCH):
                        if mc == 0:
                            pe.wait_ge(low_ready, s + 1)
                        c = s * KC + mc
                        if above(c, c - 1):
                            pe.wait_ge(max_ready, c - 1)
                        nc.tensor.matmul(ps_s[mc % 2][:], k_pair[:, j, cols], q_pair[:, j, :], start=True,
                                         stop=True).then_inc(smax_done, 1)
                    if mc == 1 and in_range(s, 1, BATCH + 1):
                        pe.wait_ge(parts_ready, 2 * s)
                        if above(s, s - 1):
                            pe.wait_ge(row_ready, s - 1)
                        for n in range(KC):
                            m = nc.tensor.transpose(ps_n[0:2, n * P:(n + 1) * P],
                                                    negmax_parts[:, (j - 1) % 2, n, :], identh[:])
                        m.then_inc(parts_t, 1)
                for n in range(KC):
                    attend(s, j, n)
                if j % 2 == 1 and in_range(s, 5, BATCH + 5):
                    t = (s - 5) // 2
                    pe.wait_ge(un_ready, s - 3)
                    if above(s, t):
                        pe.wait_ge(x_added, t)
                    for n in range(KC):
                        m = nc.tensor.transpose(ps_x[:, n * P:(n + 1) * P],
                                                un[:, ((j - 5) % 4) // 2, n, :], ident[:])
                    m.then_inc(un_t, 1)

            run(pe, slot, 0, BATCH + 4, peel=8)


def feed_forward(nc, keep, ag_d, au_d, ad_d, out_d):
    acc, xth, xtl, ffn_w, ident = keep["acc"], keep["xth"], keep["xtl"], keep["ffn_w"], keep["ident"]
    GT = 4
    GROUPS = TILES // GT
    GTOK = GT * P
    T_AT = {3 + 2 * i: i for i in range(GT)}
    w_gate = ffn_w[:, 0:KC * INTER].rearrange("p (k i) -> p k i", k=KC)
    w_up = ffn_w[:, KC * INTER:2 * KC * INTER].rearrange("p (k i) -> p k i", k=KC)
    w_down = ffn_w[:, 2 * KC * INTER:FFN_W].rearrange("p (c h) -> p c h", c=IC)
    with ExitStack() as ctx:
        def sb(name, shape, dt):
            return ctx.enter_context(nc.sbuf_tensor(name, shape, dt))

        def sem(name):
            return ctx.enter_context(nc.semaphore(name))

        stats = keep["stats"]
        meanvar = sb("meanvar2", [P, TILES, 2], F32)
        work = sb("work2", [P, 4, TILES], F32)
        rstd = sb("rstd2", [P, TILES], F32)
        stats3 = sb("stats3", [P, GT, 6], F32)
        meanvar3 = sb("meanvar3", [P, GT, 2], F32)
        work3 = sb("work3", [P, 4, GT], F32)
        rstd3 = sb("rstd3", [P, GT], F32)
        ag = sb("ag", [P, IC], F32)
        au = sb("au", [P, IC], F32)
        ad = sb("ad", [P, HID], F32)
        gate = sb("gate", [P, 2, GTOK], F32)
        h32 = sb("h32", [P, 2, GTOK], F32)
        hh = sb("hh", [P, 2, GTOK], F16)
        hl = sb("hl", [P, 2, GTOK], F16)
        y = sb("y", [P, GT, HID], F32)
        staged = sb("staged", [P, 2, HID], F32)

        banks = [ctx.enter_context(nc.psum_tensor(f"ps_c{i}", [P, 512], F32)) for i in range(8)]
        ps_g, ps_u, ps_t, ps_d = banks[0:2], banks[2], banks[3], banks[4:8]

        stat, root, stat3, root3 = sem("stat2"), sem("root2"), sem("stat3"), sem("root3")
        small_in = sem("small_in")
        x2_ready, x2_t, x2h_ready, x2l_ready = sem("x2_ready"), sem("x2_t"), sem("x2h_ready"), sem("x2l_ready")
        gu_done, gate_ready, h32_ready, hh_ready, hl_ready = (
            sem("gu_done"), sem("gate_ready"), sem("h32_ready"), sem("hh_ready"), sem("hl_ready"))
        down_done, y_ready, y_added, y_stats = sem("down_done"), sem("y_ready"), sem("y_added"), sem("y_stats")
        x3_ready, out_sent = sem("x3_ready"), sem("out_sent")
        block = ctx.enter_context(nc.Block())

        def rows(ic):
            return P if ic < IC - 1 else ILAST

        def tile_of(t):
            return acc[:, bass.ds(t, 1), :].rearrange("p a f -> p (a f)")

        @block.sync
        def _(sp):
            with nc.allow_non_contiguous_dma("one column per chunk"):
                for v, src in ((ag, ag_d), (au, au_d)):
                    sp.dma_start(v[:, 0:IC - 1], src[0:(IC - 1) * P].rearrange("(c p) -> p c", p=P)
                                 ).then_inc(small_in, 16)
                    sp.dma_start(v[0:ILAST, IC - 1:IC], src[(IC - 1) * P:INTER].rearrange("(p c) -> p c", c=1)
                                 ).then_inc(small_in, 16)
            sp.dma_start(ad[:], ad_d.rearrange("(a f) -> a f", a=1).to_broadcast([P, HID])).then_inc(small_in, 16)
            with sp.Fori(0, TILES, 1) as t:
                sp.wait_ge(x3_ready, t + 1)
                sp.dma_start(out_d[bass.ds(t, 1), :, :].rearrange("a p f -> p (a f)"), tile_of(t)
                             ).then_inc(out_sent, 16)
            sp.wait_ge(out_sent, 16 * TILES)

        @block.gpsimd
        def _(pool):
            for t in range(TILES - GT, TILES):
                pool.wait_ge(y_ready, t + 1)
                nc.gpsimd.tensor_tensor(tile_of(t), y[:, t % GT, :], tile_of(t), ALU.add).then_inc(y_added, 1)

        @block.scalar
        def _(act):
            act.wait_ge(stat, TILES + 1)
            nc.scalar.activation(work[:, 1, :], work[:, 0, :], ACT.Sqrt).then_inc(root, 1)

            def high(t, bank=ps_t):
                act.wait_ge(x2_t, t + 1)
                nc.scalar.activation(xth[:, :, bass.ds(t * P, P)], bank[:].rearrange("p (k c) -> p k c", k=KC),
                                     ACT.Copy).then_inc(x2h_ready, 1)

            def root_of(g):
                act.wait_ge(stat3, 10 * g + GT + 1)
                nc.scalar.activation(work3[:, 1, :], work3[:, 0, :], ACT.Sqrt).then_inc(root3, 1)

            def group(g, finish, prepare):
                for ic in range(IC):
                    r, par = rows(ic), ic % 2
                    u = g * IC + ic
                    act.wait_ge(gu_done, u + 1)
                    nc.scalar.activation(gate[0:r, par, :], ps_g[par][0:r, :], ACT.Silu,
                                         scale=ag[0:r, ic:ic + 1]).then_inc(gate_ready, 1)
                    act.wait_ge(h32_ready, u + 1)
                    nc.scalar.activation(hh[0:r, par, :], h32[0:r, par, :], ACT.Copy).then_inc(hh_ready, 1)
                    if prepare and ic in T_AT:
                        high((g + 1) * GT + T_AT[ic])
                    if finish and ic == GT + 1:
                        root_of(g - 1)

            for t in range(GT):
                high(t, ps_d[t])
            act.wait_ge(small_in, 80)
            group(0, False, True)
            with act.Fori(1, GROUPS - 1, 1) as g:
                group(g, True, True)
            group(GROUPS - 1, True, False)
            root_of(GROUPS - 1)

        @block.vector
        def _(dve):
            n = norm_variance(nc, dve, stats, meanvar, work, stat, 0)
            dve.wait_ge(root, 1)
            norm_rstd(nc, dve, rstd, work, stat, n)

            def norm_staged(t, j):
                if above(t, t - 1):
                    dve.wait_ge(x2_t, t - 1)
                normalise(nc, staged[:, j, :], tile_of(t), meanvar, rstd, t).then_inc(x2_ready, 1)

            def norm(t, j):
                norm_staged(t, j)
                normalise(nc, tile_of(t), tile_of(t), meanvar, rstd, t)

            def low(t, bank=ps_t):
                dve.wait_ge(x2h_ready, t + 1)
                nc.vector.tensor_tensor(xtl[:, :, bass.ds(t * P, P)], bank[:].rearrange("p (k c) -> p k c", k=KC),
                                        xth[:, :, bass.ds(t * P, P)], ALU.subtract).then_inc(x2l_ready, 1)

            def scaled(g):
                for tt in range(GT):
                    dve.wait_ge(down_done, g * GT + tt + 1)
                    nc.vector.tensor_tensor(y[:, tt, :], ps_d[tt][:], ad[:], ALU.mult).then_inc(y_ready, 1)

            def added(g, tt):
                t = g * GT + tt
                dve.wait_ge(y_ready, t + 1)
                nc.vector.tensor_tensor(tile_of(t), y[:, tt, :], tile_of(t), ALU.add).then_inc(y_added, 1)

            def measured(g, tt):
                nc.vector.bn_stats(stats3[:, tt, :], tile_of(g * GT + tt)).then_inc(y_stats, 1)

            def variance(g):
                norm_variance(nc, dve, stats3, meanvar3, work3, stat3, 10 * g)

            def deviation(g):
                dve.wait_ge(root3, g + 1)
                norm_rstd(nc, dve, rstd3, work3, stat3, 10 * g + GT + 1)

            def send(g, tt):
                t = g * GT + tt
                normalise(nc, tile_of(t), tile_of(t), meanvar3, rstd3, tt).then_inc(x3_ready, 1)

            def group(g, finish, prepare):
                if finish:
                    scaled(g - 1)
                for ic in range(IC):
                    r, par = rows(ic), ic % 2
                    u = g * IC + ic
                    if finish and 1 <= ic <= GT:
                        dve.wait_ge(y_added, (g - 1) * GT + ic)
                    if finish and ic == GT + 1:
                        dve.wait_ge(y_stats, g * GT)
                    dve.wait_ge(gate_ready, u + 1)
                    nc.vector.scalar_tensor_tensor(h32[0:r, par, :], ps_u[0:r, :], au[0:r, ic:ic + 1],
                                                   gate[0:r, par, :], ALU.mult, ALU.mult).then_inc(h32_ready, 1)
                    dve.wait_ge(hh_ready, u + 1)
                    nc.vector.tensor_tensor(hl[0:r, par, :], h32[0:r, par, :], hh[0:r, par, :],
                                            ALU.subtract).then_inc(hl_ready, 1)
                    if prepare:
                        if ic in T_AT:
                            low((g + 1) * GT + T_AT[ic])
                        if ic + 2 in T_AT:
                            norm((g + 1) * GT + T_AT[ic + 2], T_AT[ic + 2] % 2)
                    if finish:
                        if ic < GT:
                            added(g - 1, ic)
                        if 1 <= ic <= GT:
                            measured(g - 1, ic - 1)
                        if ic == GT + 1:
                            variance(g - 1)
                        if ic == GT + 2:
                            deviation(g - 1)
                        if GT + 3 <= ic < 2 * GT + 3:
                            send(g - 1, ic - GT - 3)

            norm_staged(0, 0)
            for t in range(1, GT):
                norm_staged(t, t % 2)
                low(t - 1, ps_d[t - 1])
            low(GT - 1, ps_d[GT - 1])
            for t in range(GT):
                normalise(nc, tile_of(t), tile_of(t), meanvar, rstd, t)
            dve.wait_ge(small_in, 80)
            group(0, False, True)
            with dve.Fori(1, GROUPS - 1, 1) as g:
                group(g, True, True)
            group(GROUPS - 1, True, False)
            scaled(GROUPS - 1)
            for tt in range(GT):
                dve.wait_ge(y_added, (GROUPS - 1) * GT + tt + 1)
                measured(GROUPS - 1, tt)
            dve.wait_ge(y_stats, TILES)
            variance(GROUPS - 1)
            deviation(GROUPS - 1)
            for tt in range(GT):
                send(GROUPS - 1, tt)

        @block.tensor
        def _(pe):
            def transpose(t, j, bank=ps_t):
                pe.wait_ge(x2_ready, t + 1)
                if bank is ps_t:
                    pe.wait_ge(x2l_ready, t)
                for k in range(KC):
                    m = nc.tensor.transpose(bank[:, k * P:(k + 1) * P], staged[:, j, k * P:(k + 1) * P], ident[:])
                m.then_inc(x2_t, 1)

            def down(g, ic):
                r, par = rows(ic), ic % 2
                pe.wait_ge(hl_ready, g * IC + ic + 1)
                for tt in range(GT):
                    if ic == 0 and above(g, GT * (g - 1) + tt + 1):
                        pe.wait_ge(y_ready, GT * (g - 1) + tt + 1)
                    c = slice(tt * P, (tt + 1) * P)
                    nc.tensor.matmul(ps_d[tt][:], hh[0:r, par, c], w_down[0:r, ic, :], start=(ic == 0), stop=False)
                    m = nc.tensor.matmul(ps_d[tt][:], hl[0:r, par, c], w_down[0:r, ic, :], start=False,
                                         stop=(ic == IC - 1))
                    if ic == IC - 1:
                        m.then_inc(down_done, 1)

            def project(g, ic, out, w):
                r = rows(ic)
                c = slice(ic * P, ic * P + r)
                for k in range(KC):
                    nc.tensor.matmul(out[0:r, :], w[:, k, c], xth[:, k, bass.ds(g * GTOK, GTOK)],
                                     start=(k == 0), stop=False)
                    m = nc.tensor.matmul(out[0:r, :], w[:, k, c], xtl[:, k, bass.ds(g * GTOK, GTOK)],
                                         start=False, stop=(k == KC - 1))
                return m

            def group(g, prepare):
                pe.wait_ge(x2l_ready, GT * (g + 1))
                for ic in range(IC):
                    u = g * IC + ic
                    if prepare and ic in T_AT:
                        transpose((g + 1) * GT + T_AT[ic], T_AT[ic] % 2)
                    free = u - 1 if ic >= 2 else u - ic
                    if above(g, free):
                        pe.wait_ge(gate_ready, free)
                    project(g, ic, ps_g[ic % 2], w_gate)
                    if above(g, u):
                        pe.wait_ge(h32_ready, u)
                    project(g, ic, ps_u, w_up).then_inc(gu_done, 1)
                    if ic >= 1:
                        down(g, ic - 1)
                down(g, IC - 1)

            for t in range(GT):
                transpose(t, t % 2, ps_d[t])
            group(0, True)
            with pe.Fori(1, GROUPS - 1, 1) as g:
                group(g, True)
            group(GROUPS - 1, False)


def decoder_layer(nc, x_nat, x_t, ctx_nat, ctx_t, w_codes, w_scales, ffn_d, ag_d, au_d, ad_d,
                  cos_d, sin_d, mask_d, ident_d, out_d):
    with ExitStack() as ctx:
        def sb(name, shape, dt):
            return ctx.enter_context(nc.sbuf_tensor(name, shape, dt))

        keep = {
            "acc": sb("acc", [P, TILES, HID], F32),
            "xth": sb("xth", [P, KC, TOK], F16),
            "xtl": sb("xtl", [P, KC, TOK], F16),
            "ffn_w": sb("ffn_w", [P, FCH * CHUNK], F16),
            "ident": sb("ident", [P, P], F32),
            "stats": sb("stats", [P, TILES, 6], F32),
            "q_high": sb("q_high", [P, 4, HID], F16),
            "k_low": sb("k_low", [P, 4, HID], F16),
        }
        attention(nc, keep, x_nat, x_t, w_codes, w_scales, cos_d, sin_d, mask_d, ident_d, ffn_d)
        cross_attention(nc, keep, ctx_nat, ctx_t)
        feed_forward(nc, keep, ag_d, au_d, ad_d, out_d)


def rotary_tables():
    pos = (np.arange(P) % SEQ).astype(np.float32)
    inv_freq = (1.0 / 10000.0 ** (np.arange(0, HD, 2, dtype=np.float32) / np.float32(HD))).astype(np.float32)
    f = pos[:, None] * inv_freq[None, :]
    c = np.repeat(np.cos(f.astype(np.float64)), 2, axis=1)
    s = np.stack([-np.sin(f.astype(np.float64)), np.sin(f.astype(np.float64))], axis=-1).reshape(P, HD)
    scale = np.array([HD ** -0.5] * REP + [1.0]) / WSCALE
    return ((scale[None, :, None] * c[:, None, :]).reshape(P, ROT).astype(np.float32),
            (scale[None, :, None] * s[:, None, :]).reshape(P, ROT).astype(np.float32))


def causal_mask():
    q, k = (np.arange(P) % SEQ)[:, None], np.arange(SEQ)[None, :]
    return np.where(k <= q, 0.0, -1e30).astype(np.float32)


def pack_group(q, k, v, o):
    parts = [q.reshape(KC, -1, NKV, REP * HD), k.reshape(KC, -1, NKV, HD), v.reshape(KC, -1, NKV, HD)]
    qkv = np.concatenate(parts, axis=3).transpose(2, 1, 0, 3)
    rows = o.reshape(NKV, REP, -1, HID).transpose(0, 2, 1, 3)
    n = qkv.shape[1]
    return np.concatenate([qkv.reshape(NKV, n, -1), rows.reshape(NKV, n, -1)], axis=2)


def by_chunk(a):
    g, n, w = a.shape
    return np.ascontiguousarray(a.reshape(g, n, w // CHUNK, CHUNK).transpose(0, 2, 1, 3).reshape(-1, n, CHUNK))


def pack_ffn(wg, wu, wd):
    down = np.zeros((IC * P, HID), np.float32)
    down[:INTER] = wd.T
    cols = np.concatenate([wg.T.reshape(KC, P, INTER).transpose(1, 0, 2).reshape(P, -1),
                           wu.T.reshape(KC, P, INTER).transpose(1, 0, 2).reshape(P, -1),
                           down.reshape(IC, P, HID).transpose(1, 0, 2).reshape(P, -1),
                           np.zeros((P, FCH * CHUNK - FFN_W), np.float32)], axis=1)
    return by_chunk(cols[None])


def kernel(x, ctx_4096, L0_attn_q_codes, L0_attn_q_scales, L0_attn_k_codes, L0_attn_k_scales,
           L0_attn_v_codes, L0_attn_v_scales, L0_attn_o_codes, L0_attn_o_scales, L0_ffn_Wg, L0_ffn_Wu,
           L0_ffn_Wd, L0_ffn_ag, L0_ffn_au, L0_ffn_ad):
    import concourse.bacc as bacc
    from concourse.bass_utils import run_bass_kernel_spmd

    a = [np.asarray(v) for v in (L0_attn_q_codes, L0_attn_k_codes, L0_attn_v_codes, L0_attn_o_codes)]
    s = [np.asarray(v) for v in (L0_attn_q_scales, L0_attn_k_scales, L0_attn_v_scales, L0_attn_o_scales)]
    x, c = np.asarray(x).reshape(TOK, HID), np.asarray(ctx_4096).reshape(TOK, HID)
    cos, sin = rotary_tables()
    host = {
        "x_nat": x.reshape(TILES, P, HID),
        "x_t": x.T.reshape(KC, P, TOK),
        "ctx_nat": c.reshape(TILES, P, HID),
        "ctx_t": c.T.reshape(KC, P, TOK),
        "w_codes": by_chunk(pack_group(*a)),
        "w_scales": by_chunk(pack_group(*s)).reshape(-1, CHUNK),
        "ffn_d": pack_ffn(np.asarray(L0_ffn_Wg), np.asarray(L0_ffn_Wu), np.asarray(L0_ffn_Wd)),
        "ag_d": np.asarray(L0_ffn_ag), "au_d": np.asarray(L0_ffn_au), "ad_d": np.asarray(L0_ffn_ad),
        "cos_d": cos, "sin_d": sin, "mask_d": causal_mask(), "ident_d": np.eye(P, dtype=np.float32),
    }
    nc = bacc.Bacc("TRN2", target_bir_lowering=False, num_devices=1)
    arrays, args = {}, {}
    for name, v in host.items():
        v = np.ascontiguousarray(v)
        arrays[f"in_{name}"] = v
        args[name] = nc.dram_tensor(f"in_{name}", v.shape, mybir.dt.from_np(v.dtype), kind="ExternalInput").ap()
    args["out_d"] = nc.dram_tensor("out_0", (TILES, P, HID), F32, kind="ExternalOutput").ap()
    decoder_layer(nc, **args)
    r = run_bass_kernel_spmd(nc, [arrays], core_ids=[0])
    return r.results[0]["out_0"].reshape(BATCH, SEQ, HID)
```
